# Optimizing a Trainium2 kernel written in Bass

```python
import numpy as np
import jax
import jax.numpy as jnp

def _softmax(x, axis=-1):
    return jax.nn.softmax(x, axis=axis)

def _gelu(x):
    return jax.nn.gelu(x, approximate=True)

def _silu(x):
    return jax.nn.silu(x)

def _sigmoid(x):
    return jax.nn.sigmoid(x)

def _layernorm(x, axis=-1, eps=1e-05):
    m = jnp.mean(x, axis=axis, keepdims=True)
    v = jnp.var(x, axis=axis, keepdims=True)
    return (x - m) / jnp.sqrt(v + eps)

def _scatter_add(tgt, idx, src, axis=0):
    return tgt.at[idx].add(src)

def _segment_sum(src, seg, n):
    return jax.ops.segment_sum(src, seg, n)
kernel_name = 'mk_vit_tower_d1_tok_img512_r4_fbbe28'

def setup_inputs(seed: int=0):
    np.random.seed(seed)
    _w = jnp.asarray

    def _rec_inputs():
        import jax
        import jax.numpy as jnp
        _rk = jax.random.key(seed)
        x = -0.000392918 + 0.999932 * jax.random.normal(jax.random.fold_in(_rk, 1), (8, 1, 128, 128), jnp.float32)
        return x
    x = _rec_inputs()

    def _L0_tok_setup():
        import math
        import jax, jax.numpy as jnp
        import numpy as np
        PW = PH = 16
        EMB = 128
        HID = 128
        B, H, W = (64, 128, 128)
        L = H // PW * (W // PH)
        SIGMA_ZERO = 0.1

        def _f_noise(x):
            return jnp.sign(x) * jnp.sqrt(jnp.abs(x))

        def _noisy_linear(x, w, b, sw, sb, eps_in, eps_out):
            ei = _f_noise(eps_in)
            eo = _f_noise(eps_out)
            w_n = w + sw * (eo[:, None] * ei[None, :])
            b_n = b + sb * eo
            return x @ w_n.T + b_n

        def _unfold_patches(x):
            b = x.shape[0]
            p = x.reshape(b, H // PW, PW, W // PH, PH)
            p = p.transpose(0, 1, 3, 2, 4)
            return p.reshape(b, L, PW * PH)

        def _pos_encoding(x):
            pos = jnp.arange(L, dtype=jnp.float32)[:, None]
            div = jnp.exp(jnp.arange(0, EMB, 2, dtype=jnp.float32) * (-math.log(10000.0) / EMB))
            ang = pos * div
            pe = jnp.stack([jnp.sin(ang), jnp.cos(ang)], axis=-1).reshape(L, EMB)
            return x + pe[None, :, :]
        key = jax.random.key(seed)
        ks = jax.random.split(key, 12)
        in_f = PW * PH
        sig = SIGMA_ZERO / math.sqrt(in_f)
        bnd1 = 1.0 / math.sqrt(in_f)
        bnd3 = 1.0 / math.sqrt(HID)
        u = lambda k, shape, bnd: jax.random.uniform(k, shape, jnp.float32, -bnd, bnd)
        return {'inputs': jax.random.normal(ks[0], (B, 1, H, W), jnp.float32), 'W1_w': u(ks[1], (HID, in_f), bnd1), 'W1_b': u(ks[2], (HID,), bnd1), 'W1_sw': jnp.full((HID, in_f), sig, jnp.float32), 'W1_sb': jnp.full((HID,), sig, jnp.float32), 'W2_w': u(ks[3], (HID, in_f), bnd1), 'W2_b': u(ks[4], (HID,), bnd1), 'W2_sw': jnp.full((HID, in_f), sig, jnp.float32), 'W2_sb': jnp.full((HID,), sig, jnp.float32), 'W3_w': u(ks[5], (EMB, HID), bnd3), 'W3_b': u(ks[6], (EMB,), bnd3), 'eps_in1': jax.random.normal(ks[7], (in_f,), jnp.float32), 'eps_out1': jax.random.normal(ks[8], (HID,), jnp.float32), 'eps_in2': jax.random.normal(ks[9], (in_f,), jnp.float32), 'eps_out2': jax.random.normal(ks[10], (HID,), jnp.float32)}
    _L0_tok_all = _L0_tok_setup()
    _L0_tok_in = {k: v for k, v in _L0_tok_all.items() if k in ('W1_w', 'W1_b', 'W1_sw', 'W1_sb', 'W2_w', 'W2_b', 'W2_sw', 'W2_sb', 'W3_w', 'W3_b', 'eps_in1', 'eps_out1', 'eps_in2', 'eps_out2')}
    del _L0_tok_all

    def _L0_attn_setup():
        import jax, jax.numpy as jnp
        import numpy as np
        B, N, C = (2, 1024, 128)
        NUM_HEADS = 8
        HEAD_DIM = C // NUM_HEADS
        SCALE = HEAD_DIM ** (-0.5)
        THETA = 10000.0

        def _rope(x, seq_len, head_dim):
            freqs = 1.0 / THETA ** (jnp.arange(0, head_dim, 2, dtype=jnp.float32) / head_dim)
            t = jnp.arange(seq_len, dtype=jnp.float32)
            freqs_cis = jnp.outer(t, freqs)
            sin_f = jnp.sin(freqs_cis)
            cos_f = jnp.cos(freqs_cis)
            x_even = x[..., ::2]
            x_odd = x[..., 1::2]
            rot = jnp.stack([x_even * cos_f - x_odd * sin_f, x_even * sin_f + x_odd * cos_f], axis=-1)
            return rot.reshape(x.shape)
        key = jax.random.key(seed)
        ks = jax.random.split(key, 5)
        x = jax.random.normal(ks[0], (B, N, C), dtype=jnp.float32)
        Wqkv = jax.random.normal(ks[1], (3 * C, C), dtype=jnp.float32) * 0.02
        bqkv = jax.random.normal(ks[2], (3 * C,), dtype=jnp.float32) * 0.02
        Wproj = jax.random.normal(ks[3], (C, C), dtype=jnp.float32) * 0.02
        bproj = jax.random.normal(ks[4], (C,), dtype=jnp.float32) * 0.02
        return {'x': x, 'Wqkv': Wqkv, 'bqkv': bqkv, 'Wproj': Wproj, 'bproj': bproj}
    _L0_attn_all = _L0_attn_setup()
    _L0_attn_in = {k: v for k, v in _L0_attn_all.items() if k in ('Wqkv', 'bqkv', 'Wproj', 'bproj')}
    del _L0_attn_all

    def _L0_ffn_setup():
        import jax, jax.numpy as jnp
        import numpy as np
        B, T, D, H = (2, 256, 128, 512)
        G, E = (4, 8)
        GK, EK = (2, 2)
        EPS = 1e-05
        SCALE = 0.02

        def _layernorm(x, g, b):
            m = jnp.mean(x, axis=-1, keepdims=True)
            xc = x - m
            v = jnp.mean(xc * xc, axis=-1, keepdims=True)
            return xc * jax.lax.rsqrt(v + EPS) * g + b

        def _topk_gate(logits, k, n):
            v, i = jax.lax.top_k(logits, k)
            sc = jax.nn.softmax(v, axis=-1)
            return jnp.sum(jax.nn.one_hot(i, n, dtype=logits.dtype) * sc[..., None], axis=-2)
        key = jax.random.key(seed)
        ks = jax.random.split(key, 6)
        return {'inp': jax.random.normal(ks[0], (B, T, D), jnp.float32), 'ln_g': jnp.ones((D,), jnp.float32), 'ln_b': jnp.zeros((D,), jnp.float32), 'wg_group': jax.random.normal(ks[1], (D, G), jnp.float32) * SCALE, 'wg_inner': jax.random.normal(ks[2], (G, D, E), jnp.float32) * SCALE, 'W1': jax.random.normal(ks[3], (G, E, D, H), jnp.float32) * SCALE, 'b1': jnp.zeros((G, E, H), jnp.float32), 'W2': jax.random.normal(ks[4], (G, E, H, D), jnp.float32) * SCALE, 'b2': jnp.zeros((G, E, D), jnp.float32), 'gln_g': jnp.ones((G, D), jnp.float32), 'gln_b': jnp.zeros((G, D), jnp.float32)}
    _L0_ffn_all = _L0_ffn_setup()
    _L0_ffn_in = {k: v for k, v in _L0_ffn_all.items() if k in ('ln_g', 'ln_b', 'wg_group', 'wg_inner', 'W1', 'b1', 'W2', 'b2', 'gln_g', 'gln_b')}
    del _L0_ffn_all
    return {'x': x, 'L0_tok_W1_w': _L0_tok_in['W1_w'], 'L0_tok_W1_b': _L0_tok_in['W1_b'], 'L0_tok_W1_sw': _L0_tok_in['W1_sw'], 'L0_tok_W1_sb': _L0_tok_in['W1_sb'], 'L0_tok_W2_w': _L0_tok_in['W2_w'], 'L0_tok_W2_b': _L0_tok_in['W2_b'], 'L0_tok_W2_sw': _L0_tok_in['W2_sw'], 'L0_tok_W2_sb': _L0_tok_in['W2_sb'], 'L0_tok_W3_w': _L0_tok_in['W3_w'], 'L0_tok_W3_b': _L0_tok_in['W3_b'], 'L0_tok_eps_in1': _L0_tok_in['eps_in1'], 'L0_tok_eps_out1': _L0_tok_in['eps_out1'], 'L0_tok_eps_in2': _L0_tok_in['eps_in2'], 'L0_tok_eps_out2': _L0_tok_in['eps_out2'], 'L0_attn_Wqkv': _L0_attn_in['Wqkv'], 'L0_attn_bqkv': _L0_attn_in['bqkv'], 'L0_attn_Wproj': _L0_attn_in['Wproj'], 'L0_attn_bproj': _L0_attn_in['bproj'], 'L0_ffn_ln_g': _L0_ffn_in['ln_g'], 'L0_ffn_ln_b': _L0_ffn_in['ln_b'], 'L0_ffn_wg_group': _L0_ffn_in['wg_group'], 'L0_ffn_wg_inner': _L0_ffn_in['wg_inner'], 'L0_ffn_W1': _L0_ffn_in['W1'], 'L0_ffn_b1': _L0_ffn_in['b1'], 'L0_ffn_W2': _L0_ffn_in['W2'], 'L0_ffn_b2': _L0_ffn_in['b2'], 'L0_ffn_gln_g': _L0_ffn_in['gln_g'], 'L0_ffn_gln_b': _L0_ffn_in['gln_b']}

def reference(x, L0_tok_W1_w, L0_tok_W1_b, L0_tok_W1_sw, L0_tok_W1_sb, L0_tok_W2_w, L0_tok_W2_b, L0_tok_W2_sw, L0_tok_W2_sb, L0_tok_W3_w, L0_tok_W3_b, L0_tok_eps_in1, L0_tok_eps_out1, L0_tok_eps_in2, L0_tok_eps_out2, L0_attn_Wqkv, L0_attn_bqkv, L0_attn_Wproj, L0_attn_bproj, L0_ffn_ln_g, L0_ffn_ln_b, L0_ffn_wg_group, L0_ffn_wg_inner, L0_ffn_W1, L0_ffn_b1, L0_ffn_W2, L0_ffn_b2, L0_ffn_gln_g, L0_ffn_gln_b):
    import jax
    import jax.numpy as jnp

    def _L0_tok_ref(inputs, W1_w, W1_b, W1_sw, W1_sb, W2_w, W2_b, W2_sw, W2_sb, W3_w, W3_b, eps_in1, eps_out1, eps_in2, eps_out2):
        import math
        import jax, jax.numpy as jnp
        import numpy as np
        PW = PH = 16
        EMB = 128
        HID = 128
        B, H, W = (64, 128, 128)
        L = H // PW * (W // PH)
        SIGMA_ZERO = 0.1

        def _f_noise(x):
            return jnp.sign(x) * jnp.sqrt(jnp.abs(x))

        def _noisy_linear(x, w, b, sw, sb, eps_in, eps_out):
            ei = _f_noise(eps_in)
            eo = _f_noise(eps_out)
            w_n = w + sw * (eo[:, None] * ei[None, :])
            b_n = b + sb * eo
            return x @ w_n.T + b_n

        def _unfold_patches(x):
            b = x.shape[0]
            p = x.reshape(b, H // PW, PW, W // PH, PH)
            p = p.transpose(0, 1, 3, 2, 4)
            return p.reshape(b, L, PW * PH)

        def _pos_encoding(x):
            pos = jnp.arange(L, dtype=jnp.float32)[:, None]
            div = jnp.exp(jnp.arange(0, EMB, 2, dtype=jnp.float32) * (-math.log(10000.0) / EMB))
            ang = pos * div
            pe = jnp.stack([jnp.sin(ang), jnp.cos(ang)], axis=-1).reshape(L, EMB)
            return x + pe[None, :, :]
        x = _unfold_patches(inputs)
        g = _noisy_linear(x, W1_w, W1_b, W1_sw, W1_sb, eps_in1, eps_out1)
        x_gate = g * jnp.tanh(jax.nn.softplus(g))
        x_inner = _noisy_linear(x, W2_w, W2_b, W2_sw, W2_sb, eps_in2, eps_out2)
        x = x_gate * x_inner
        x = x @ W3_w.T + W3_b
        return _pos_encoding(x)

    def _L0_attn_ref(x, Wqkv, bqkv, Wproj, bproj):
        import jax, jax.numpy as jnp
        import numpy as np
        B, N, C = (2, 1024, 128)
        NUM_HEADS = 8
        HEAD_DIM = C // NUM_HEADS
        SCALE = HEAD_DIM ** (-0.5)
        THETA = 10000.0

        def _rope(x, seq_len, head_dim):
            freqs = 1.0 / THETA ** (jnp.arange(0, head_dim, 2, dtype=jnp.float32) / head_dim)
            t = jnp.arange(seq_len, dtype=jnp.float32)
            freqs_cis = jnp.outer(t, freqs)
            sin_f = jnp.sin(freqs_cis)
            cos_f = jnp.cos(freqs_cis)
            x_even = x[..., ::2]
            x_odd = x[..., 1::2]
            rot = jnp.stack([x_even * cos_f - x_odd * sin_f, x_even * sin_f + x_odd * cos_f], axis=-1)
            return rot.reshape(x.shape)
        b, n, c = x.shape
        qkv = x @ Wqkv.T + bqkv
        qkv = qkv.reshape(b, n, 3, NUM_HEADS, HEAD_DIM)
        qkv = jnp.transpose(qkv, (2, 0, 3, 1, 4))
        q, k, v = (qkv[0], qkv[1], qkv[2])
        q = _rope(q, n, HEAD_DIM)
        k = _rope(k, n, HEAD_DIM)
        attn = jnp.einsum('bhqd,bhkd->bhqk', q, k) * SCALE
        attn = jax.nn.softmax(attn, axis=-1)
        out = jnp.einsum('bhqk,bhkd->bhqd', attn, v)
        out = jnp.transpose(out, (0, 2, 1, 3)).reshape(b, n, c)
        return out @ Wproj.T + bproj

    def _L0_ffn_ref(inp, ln_g, ln_b, wg_group, wg_inner, W1, b1, W2, b2, gln_g, gln_b):
        import jax, jax.numpy as jnp
        import numpy as np
        B, T, D, H = (2, 256, 128, 512)
        G, E = (4, 8)
        GK, EK = (2, 2)
        EPS = 1e-05
        SCALE = 0.02

        def _layernorm(x, g, b):
            m = jnp.mean(x, axis=-1, keepdims=True)
            xc = x - m
            v = jnp.mean(xc * xc, axis=-1, keepdims=True)
            return xc * jax.lax.rsqrt(v + EPS) * g + b

        def _topk_gate(logits, k, n):
            v, i = jax.lax.top_k(logits, k)
            sc = jax.nn.softmax(v, axis=-1)
            return jnp.sum(jax.nn.one_hot(i, n, dtype=logits.dtype) * sc[..., None], axis=-2)
        b, t, d = inp.shape
        x = inp.reshape(-1, d)
        gw = _topk_gate(x @ wg_group, GK, G)
        z = _layernorm(x, ln_g, ln_b)
        out = jnp.zeros_like(x)
        for g in range(G):
            iw = _topk_gate(z @ wg_inner[g], EK, E)
            moe = jnp.zeros_like(z)
            for e in range(E):
                h = jax.nn.relu(z @ W1[g, e] + b1[g, e])
                moe = moe + iw[:, e:e + 1] * (h @ W2[g, e] + b2[g, e])
            y = _layernorm(z + moe, gln_g[g], gln_b[g])
            out = out + gw[:, g:g + 1] * y
        return out.reshape(b, t, d) + inp
    h = _L0_tok_ref(x, L0_tok_W1_w, L0_tok_W1_b, L0_tok_W1_sw, L0_tok_W1_sb, L0_tok_W2_w, L0_tok_W2_b, L0_tok_W2_sw, L0_tok_W2_sb, L0_tok_W3_w, L0_tok_W3_b, L0_tok_eps_in1, L0_tok_eps_out1, L0_tok_eps_in2, L0_tok_eps_out2)
    h = h + _L0_attn_ref(_layernorm(h, axis=-1), L0_attn_Wqkv, L0_attn_bqkv, L0_attn_Wproj, L0_attn_bproj)
    h = h + _L0_ffn_ref(_layernorm(h, axis=-1), L0_ffn_ln_g, L0_ffn_ln_b, L0_ffn_wg_group, L0_ffn_wg_inner, L0_ffn_W1, L0_ffn_b1, L0_ffn_W2, L0_ffn_b2, L0_ffn_gln_g, L0_ffn_gln_b)
    return h

_drawn_inputs = setup_inputs


def setup_inputs(seed=0):
    import zlib

    import numpy as np

    out = dict(_drawn_inputs(seed))
    spreads = {'L0_tok_W1_sw': (0.0062500000931322575, 0.6),
     'L0_tok_W1_sb': (0.0062500000931322575, 0.6),
     'L0_tok_W2_sw': (0.0062500000931322575, 0.6),
     'L0_tok_W2_sb': (0.0062500000931322575, 0.6),
     'L0_ffn_ln_g': (1.0, 0.2),
     'L0_ffn_ln_b': (0.0, 0.1),
     'L0_ffn_b1': (0.0, 0.8),
     'L0_ffn_b2': (0.0, 0.432),
     'L0_ffn_gln_g': (1.0, 0.2),
     'L0_ffn_gln_b': (0.0, 0.271)}
    factors = {'L0_tok_W1_b': 4.098,
     'L0_tok_W2_b': 4.161,
     'L0_attn_bqkv': 6.412,
     'L0_ffn_wg_inner': 2.676,
     'L0_ffn_W1': 4.802,
     'L0_ffn_W2': 3.766}
    for name, (base, spread) in spreads.items():
        noise = np.random.default_rng([zlib.crc32(name.encode()), seed]).standard_normal(out[name].shape)
        drawn = base * np.exp(spread * noise) if base else spread * noise
        out[name] = jnp.asarray(drawn.astype(out[name].dtype))
    for name, factor in factors.items():
        out[name] = (out[name] * factor).astype(out[name].dtype)
    return out
```

```python
from contextlib import ExitStack

import numpy as np

import concourse.bass as bass
from concourse import mybir

F32 = mybir.dt.float32
F16 = mybir.dt.float16
ALU = mybir.AluOpType
ACT = mybir.ActivationFunctionType
AX = mybir.AxisListType

P = 128
IMG, PIX, PATCH = 8, 128, 16
SIDE = PIX // PATCH
L = SIDE * SIDE
N = IMG * L
NC = N // P
FEAT = PATCH * PATCH
KF = FEAT // P
D = 128
HEADS = 8
HD = D // HEADS
G, E, H = 4, 8, 512
HC = H // P
SETS = G + 1
EPS = 1e-5
TINY = 2.0 ** -60
WCOLS = HC + 2 * H
WSPLIT = 4
STEPS = E * HC
LAG = 3


def columns(parts):
    at, where = 0, {}
    for name, width in parts:
        where[name] = slice(at, at + width)
        at += width
    return where, at


TOK_PARTS = [("noise_in", KF * 2), ("noise_out", 2), ("noise_row", 2 * D), ("b", 2), ("sb", 2), ("w", KF * 2 * D),
             ("sw", KF * 2 * D), ("xT", KF * N)]
MID_PARTS = [("w3T", D), ("b3", D), ("pe", D), ("ident", D), ("wqkvT", 5 * D), ("bqkv", 4), ("bv", 1),
             ("cos", L), ("sin", L), ("headmask", HEADS), ("parmask", D), ("wprojT", D), ("bproj", D)]
FFN_PARTS = [("wg", G), ("wgi", G * E), ("ln_g", 1), ("ln_b", 1), ("order", E), ("gln_g", G * D), ("gln_b", D),
             ("b2", G * D)]
TOK_AT, TOK_W = columns(TOK_PARTS)
MID_AT, MID_W = columns(MID_PARTS)
FFN_AT, FFN_W = columns(FFN_PARTS)


def vit_tower(nc, tok_in, mid_in, ffn_in, experts, out):
    ctx = ExitStack()
    with ctx:
        def sb(name, shape, dt=F32):
            return ctx.enter_context(nc.sbuf_tensor(name, shape, dt))

        def sem(name):
            return ctx.enter_context(nc.semaphore(name))

        bank = [ctx.enter_context(nc.psum_tensor(f"bank{i}", [P, 512], F32)) for i in range(8)]
        gates_dram = nc.dram_tensor("gates_t", [G * E, N], F32)

        tok = sb("tok", [P, TOK_W])
        mid = sb("mid", [P, MID_W])
        ffn = sb("ffn", [P, FFN_W])

        def tk(name):
            return tok[:, TOK_AT[name]]

        def md(name):
            return mid[:, MID_AT[name]]

        def ff(name):
            return ffn[:, FFN_AT[name]]

        NOISE = KF * 2 + 2 + 2 * D
        noise_abs = sb("noise_abs", [P, NOISE])
        noise_log = sb("noise_log", [P, NOISE])
        noise_f = sb("noise_f", [P, NOISE])
        w_noise = sb("w_noise", [P, KF * 2 * D])
        w_noisy = sb("w_noisy", [P, KF * 2 * D])
        b_noisy = sb("b_noisy", [P, 2])
        gate_in = sb("gate_in", [P, N])
        gate_cap = sb("gate_cap", [P, N])
        gate_u = sb("gate_u", [P, N])
        gate_n = sb("gate_n", [P, N])
        gate_d = sb("gate_d", [P, N])
        gate_r = sb("gate_r", [P, N])
        gated = sb("gated", [P, N])
        pe_b3 = sb("pe_b3", [P, D])
        h0 = sb("h0", [P, NC, D])
        h0_bproj = sb("h0_bproj", [P, NC, D])
        stats = sb("stats", [P, NC, 6])
        mv = sb("mv", [P, NC, 2])
        small = sb("small", [P, 8, NC])
        xhat = sb("xhat", [P, NC, D])
        xhatT = sb("xhatT", [P, N])
        rot_a = sb("rot_a", [P, 2, N])
        rot_b = sb("rot_b", [P, 2, N])
        qkT = sb("qkT", [P, 2, N])
        k_heads = sb("k_heads", [P, IMG, HEADS, L])
        v_heads = sb("v_heads", [P, IMG, D])
        row_max = sb("row_max", [P, NC, HEADS])
        row_sum = sb("row_sum", [P, NC, HEADS])
        row_inv = sb("row_inv", [P, NC, HEADS])
        shifted = sb("shifted", [P, NC, HEADS * L])
        probs = sb("probs", [P, NC, HEADS * L])
        probs_n = sb("probs_n", [P, NC, HEADS * L])
        probsT = sb("probsT", [P, NC, 512])
        attnT = sb("attnT", [P, N])
        h1 = sb("h1", [P, NC, D])
        inp = sb("inp", [P, NC, D])
        zhat = sb("zhat", [P, NC, D])
        inpT = sb("inpT", [P, N])
        zT = sb("zT", [P, N])
        z_hi = sb("z_hi", [P, N], F16)
        z_lo = sb("z_lo", [P, N], F16)
        logits = sb("logits", [P, NC, SETS, E])
        rest = sb("rest", [P, NC, SETS, E])
        equal = sb("equal", [P, NC, SETS, E])
        key = sb("key", [P, NC, SETS, E])
        first = sb("first", [P, NC, SETS, E])
        second = sb("second", [P, NC, SETS, E])
        gates = sb("gates", [P, NC, SETS, E])
        top = sb("top", [P, 8, NC * SETS])
        gatesT = sb("gatesT", [SETS * E, N])
        out_acc = sb("out_acc", [P, NC, D])

        w_stage = sb("w_stage", [P, E, WCOLS])
        w_hi = sb("w_hi", [P, WSPLIT, 2 * H], F16)
        w_lo = sb("w_lo", [P, WSPLIT, 2 * H], F16)
        iw_rows = k_heads[:].rearrange("p b h k -> p (b h k)").rearrange("p (e n) -> p e n", e=E)
        relu = probs[:]
        h_hi = shifted[:].rearrange("p c n -> p (c n)").bitcast(F16).rearrange("p (t c n) -> p t c n", t=2, c=HC)
        h_lo = probs_n[:].rearrange("p c n -> p (c n)").bitcast(F16).rearrange("p (t c n) -> p t c n", t=2, c=HC)
        o_gated = sb("o_gated", [P, 2, N])
        moeT = sb("moeT", [P, G, N])
        moe_sumT = sb("moe_sumT", [P, N])
        y_stats = sb("y_stats", [P, NC, 6])
        y_mv = sb("y_mv", [P, NC, 2])
        y_small = sb("y_small", [P, 6, NC])
        y_hat = sb("y_hat", [P, NC, D])
        y_scaled = sb("y_scaled", [P, NC, D])

        tok_landed, mid_landed, ffn_landed = sem("tok_landed"), sem("mid_landed"), sem("ffn_landed")
        w_landed = [sem(f"w_landed{i}") for i in range(E)]
        iw_landed = [sem(f"iw_landed{i}") for i in range(E)]
        gates_stored, out_stored = sem("gates_stored"), sem("out_stored")
        dve_chain, act_chain, pool_chain = sem("dve_chain"), sem("act_chain"), sem("pool_chain")
        noise_ready, noise_root = sem("noise_ready"), sem("noise_root")
        weights_noisy = sem("weights_noisy")
        gate_mm, inner_mm = sem("gate_mm"), sem("inner_mm")
        cap_ready, u_ready = sem("cap_ready"), sem("u_ready")
        gated_ready, h0_mm, h0_ready = sem("gated_ready"), sem("h0_mm"), sem("h0_ready")
        h0b_ready = sem("h0b_ready")
        var_ready, root_ready = sem("var_ready"), sem("root_ready")
        xhat_ready, xhatT_mm, xhatT_ready = sem("xhat_ready"), sem("xhatT_mm"), sem("xhatT_ready")
        qk_mm, v_mm = sem("qk_mm"), sem("v_mm")
        rot_ready, qk_ready = sem("rot_ready"), sem("qk_ready")
        k_heads_dve, k_heads_act, v_ready = sem("k_heads_dve"), sem("k_heads_act"), sem("v_ready")
        scores_mm, shifted_ready, probs_ready = sem("scores_mm"), sem("shifted_ready"), sem("probs_ready")
        inv_ready, probs_normed = sem("inv_ready"), sem("probs_normed")
        probsT_mm, probsT_ready = sem("probsT_mm"), sem("probsT_ready")
        attn_mm, attn_ready, proj_mm = sem("attn_mm"), sem("attn_ready"), sem("proj_mm")
        inp_ready, inpT_mm, inpT_ready = sem("inp_ready"), sem("inpT_mm"), sem("inpT_ready")
        zhat_ready, zT_mm, zT_ready = sem("zhat_ready"), sem("zT_mm"), sem("zT_ready")
        z_hi_ready, z_lo_ready = sem("z_hi_ready"), sem("z_lo_ready")
        logits_mm, gap_ready, gap_exp = sem("logits_mm"), sem("gap_ready"), sem("gap_exp")
        gates_ready, gatesT_mm, gatesT_ready = sem("gates_ready"), sem("gatesT_mm"), sem("gatesT_ready")
        b2_mm, moe_seeded, seed_out_mm = sem("b2_mm"), sem("moe_seeded"), sem("seed_out_mm")
        w_hi_ready, w_lo_ready = sem("w_hi_ready"), sem("w_lo_ready")
        up_done, relu_done = sem("up_done"), sem("relu_done")
        hi_done, split_done, down_done = sem("hi_done"), sem("split_done"), sem("down_done")
        o_gated_ready, o_summed = sem("o_gated_ready"), sem("o_summed")
        yT_mm, y_var_ready, y_root_ready, yT_read = sem("yT_mm"), sem("y_var_ready"), sem("y_root_ready"), sem("yT_read")
        out_ready = sem("out_ready")
        held = sem("held")

        ident = md("ident")

        block = ctx.enter_context(nc.Block())

        def wide(ap, shape):
            return ap.to_broadcast(shape)

        @block.sync
        def _(sync):
            sync.dma_start(tok[:], tok_in).then_inc(tok_landed, 16)
            sync.dma_start(mid[:], mid_in).then_inc(mid_landed, 16)
            sync.dma_start(w_stage[:, 0, :], experts[0]).then_inc(w_landed[0], 16)
            sync.dma_start(ffn[:], ffn_in).then_inc(ffn_landed, 16)
            for e in range(1, E):
                sync.dma_start(w_stage[:, e, :], experts[e]).then_inc(w_landed[e], 16)
            sync.wait_ge(gatesT_ready, 1)
            sync.dma_start(gates_dram[:, :], gatesT[0:G * E, :]).then_inc(gates_stored, 16)
            sync.wait_ge(gates_stored, 16)
            for e in range(E):
                sync.dma_start(iw_rows[:, e, :], gates_dram[e:e + 1, :].to_broadcast([P, N])).then_inc(iw_landed[e], 16)
            with sync.Fori(1, G) as g:
                for e in range(E):
                    expert = sync.snap(g * E + e)
                    through, biased = sync.snap(g * E + (e + 1 - E)), sync.snap(g * STEPS + (HC * (e + 1) - STEPS))
                    sync.wait_ge(relu_done, biased)
                    sync.sem_inc(held, 1)
                    sync.dma_start(w_stage[:, e, :], experts[bass.ds(expert, 1), :, :].squeeze(0)).then_inc(w_landed[e], 16)
                    sync.wait_ge(o_gated_ready, through)
                    sync.sem_inc(held, 1)
                    sync.dma_start(iw_rows[:, e, :], gates_dram[bass.ds(expert, 1), :].to_broadcast([P, N])).then_inc(iw_landed[e], 16)
            for e in range(2):
                sync.wait_ge(w_lo_ready, (G - 1) * E + e + 1)
                sync.wait_ge(relu_done, (G - 1) * STEPS + HC * (e + 1))
                sync.dma_start(w_stage[:, e, 0:HC], experts[e, :, 0:HC]).then_inc(w_landed[e], 16)
            sync.wait_ge(out_ready, 1)
            sync.dma_start(out.rearrange("(c p) d -> p c d", p=P), out_acc[:]).then_inc(out_stored, 16)
            sync.wait_ge(out_stored, 16)

        @block.tensor
        def _(pe):
            pe.wait_ge(tok_landed, 16)
            pe.wait_ge(weights_noisy, 1)
            wn = w_noisy[:].rearrange("p (k w h) -> p k w h", k=KF, w=2)
            xT = tk("xT").rearrange("p (k n) -> p k n", k=KF)
            for w, done in ((0, gate_mm), (1, inner_mm)):
                for k in range(KF):
                    mm = nc.tensor.matmul(bank[w][:], wn[:, k, w, :], xT[:, k, :], start=(k == 0), stop=(k == KF - 1))
                mm.then_inc(done, 1)
            pe.wait_ge(mid_landed, 16)
            pe.wait_ge(gated_ready, 1)
            for c in range(NC):
                mm = nc.tensor.matmul(bank[2][:, c * P:(c + 1) * P], gated[:, c * P:(c + 1) * P], md("w3T"), start=True, stop=True)
            mm.then_inc(h0_mm, 1)
            for c in range(NC):
                pe.wait_ge(xhat_ready, c + 1)
                mm = nc.tensor.transpose(bank[3][:, c * P:(c + 1) * P], xhat[:, c, :], ident)
            mm.then_inc(xhatT_mm, 1)
            pe.wait_ge(xhatT_ready, 1)
            for i in range(4):
                w = mid[:, MID_AT["wqkvT"].start + i * D:MID_AT["wqkvT"].start + (i + 1) * D]
                nc.tensor.matmul(bank[4 + i][:], w, xhatT[:], start=True, stop=True).then_inc(qk_mm, 1)
            wv = mid[:, MID_AT["wqkvT"].start + 4 * D:MID_AT["wqkvT"].start + 5 * D]
            for b in range(IMG):
                for half in range(2):
                    mm = nc.tensor.matmul(bank[b // 4][half * L:(half + 1) * L, (b % 4) * D:(b % 4 + 1) * D],
                                          xhatT[:, b * L:(b + 1) * L], wv, start=True, stop=True)
                if b % 4 == 3:
                    mm.then_inc(v_mm, 1)
            pe.wait_ge(qk_ready, 2)
            pe.wait_ge(k_heads_dve, HEADS // 2)
            pe.wait_ge(k_heads_act, HEADS // 2)
            pe.wait_ge(h0_ready, 1)
            for c in range(NC):
                for half in range(2):
                    b = 2 * c + half
                    mm = nc.tensor.matmul(bank[2 + c][half * L:(half + 1) * L, :], qkT[:, 0, b * L:(b + 1) * L],
                                          k_heads[:, b].rearrange("p h k -> p (h k)"), start=True, stop=True)
                mm.then_inc(scores_mm, 1)
            pt_bank = [6, 7, 0, 1]
            pe.wait_ge(v_ready, 2)
            for c in range(NC):
                pe.wait_ge(probs_normed, c + 1)
                for hp in range(4):
                    mm = nc.tensor.transpose(bank[pt_bank[c]][:, hp * P:(hp + 1) * P], probs_n[:, c, hp * P:(hp + 1) * P], ident)
                mm.then_inc(probsT_mm, 1)
            for c in range(NC):
                pe.wait_ge(probsT_ready, c + 1)
                for half in range(2):
                    b = 2 * c + half
                    for hp in range(4):
                        mm = nc.tensor.matmul(bank[2][hp * 32:(hp + 1) * 32, b * L:(b + 1) * L],
                                              v_heads[:, b, hp * 32:(hp + 1) * 32],
                                              probsT[:, c, hp * P + half * L:hp * P + (half + 1) * L], start=True, stop=True)
            mm.then_inc(attn_mm, 1)
            pe.wait_ge(attn_ready, 1)
            for c in range(NC):
                mm = nc.tensor.matmul(bank[3][:, c * P:(c + 1) * P], attnT[:, c * P:(c + 1) * P], md("wprojT"), start=True, stop=True)
            mm.then_inc(proj_mm, 1)
            for c in range(NC):
                pe.wait_ge(inp_ready, c + 1)
                mm = nc.tensor.transpose(bank[4][:, c * P:(c + 1) * P], inp[:, c, :], ident)
            mm.then_inc(inpT_mm, 1)
            for c in range(NC):
                pe.wait_ge(zhat_ready, c + 1)
                mm = nc.tensor.transpose(bank[5][:, c * P:(c + 1) * P], zhat[:, c, :], ident)
            mm.then_inc(zT_mm, 1)
            pe.wait_ge(ffn_landed, 16)
            pe.wait_ge(inpT_ready, 1)
            for c in range(NC):
                nc.tensor.matmul(bank[6][:, c * G:(c + 1) * G], inpT[:, c * P:(c + 1) * P], ff("wg"), start=True, stop=True)
            pe.wait_ge(zT_ready, 1)
            for c in range(NC):
                mm = nc.tensor.matmul(bank[6][:, 128 + c * G * E:128 + (c + 1) * G * E], zT[:, c * P:(c + 1) * P], ff("wgi"), start=True, stop=True)
            mm.then_inc(logits_mm, 1)

            def up(g, s):
                e, c = divmod(s, HC)
                if c == 0:
                    pe.wait_ge(w_hi_ready, g * E + (e + 1))
                    pe.wait_ge(w_lo_ready, g * E + (e + 1))
                if not (isinstance(g, int) and g * STEPS + s < HC):
                    pe.wait_ge(relu_done, g * STEPS + (s + 1 - HC))
                cols = slice(c * P, (c + 1) * P)
                nc.tensor.matmul(bank[c][:], w_hi[:, e % WSPLIT, cols], z_hi[:], start=True, stop=False)
                nc.tensor.matmul(bank[c][:], w_hi[:, e % WSPLIT, cols], z_lo[:], start=False, stop=False)
                nc.tensor.matmul(bank[c][:], w_lo[:, e % WSPLIT, cols], z_hi[:], start=False, stop=True).then_inc(up_done, 1)

            def down(g, s):
                e, c = divmod(s, HC)
                pe.wait_ge(split_done, g * STEPS + (s + 1))
                if c == 0 and not (isinstance(g, int) and g * E + e < 2):
                    pe.wait_ge(o_gated_ready, g * E + (e - 1))
                cols = slice(H + c * D, H + (c + 1) * D)
                o = bank[4 + e % 2]
                nc.tensor.matmul(o[:], w_hi[:, e % WSPLIT, cols], h_hi[:, e % 2, c, :], start=(c == 0), stop=False)
                nc.tensor.matmul(o[:], w_hi[:, e % WSPLIT, cols], h_lo[:, e % 2, c, :], start=False, stop=False)
                nc.tensor.matmul(o[:], w_lo[:, e % WSPLIT, cols], h_hi[:, e % 2, c, :], start=False, stop=(c == HC - 1)).then_inc(down_done, 1)

            def back(g):
                pe.wait_ge(o_summed, g * E)
                for c in range(NC):
                    mm = nc.tensor.transpose(bank[6][:, c * P:(c + 1) * P],
                                             moe_sumT[:, c * P:(c + 1) * P], ident)
                mm.then_inc(yT_mm, 1)

            def seeds():
                pe.wait_ge(gates_ready, 1)
                for c in range(NC):
                    mm = nc.tensor.transpose(bank[7][0:SETS * E, c * P:(c + 1) * P], gates[:, c].rearrange("p s e -> p (s e)"), ident)
                mm.then_inc(gatesT_mm, 1)
                pe.wait_ge(gatesT_ready, 1)
                for g in range(G):
                    if g >= 2:
                        pe.wait_ge(moe_seeded, g - 1)
                    b2 = ffn[0:SETS * E, FFN_AT["b2"].start + g * D:FFN_AT["b2"].start + (g + 1) * D]
                    nc.tensor.matmul(bank[6 + g % 2][:], b2, gatesT[:], start=True, stop=True).then_inc(b2_mm, 1)
                pe.wait_ge(moe_seeded, G)
                for c in range(NC):
                    mm = nc.tensor.matmul(bank[7][:, c * P:(c + 1) * P], gatesT[:, c * P:(c + 1) * P],
                                          ffn[0:SETS * E, FFN_AT["gln_b"]], start=True, stop=True)
                mm.then_inc(seed_out_mm, 1)

            def group(g):
                for s in range(STEPS + LAG):
                    if s < STEPS:
                        if isinstance(g, int) and s == 0:
                            pe.wait_ge(z_hi_ready, 1)
                            pe.wait_ge(z_lo_ready, 1)
                        up(g, s)
                    if isinstance(g, int) and s == LAG - 1:
                        seeds()
                    if not isinstance(g, int) and s == 2 * HC:
                        back(g)
                    if s >= LAG:
                        down(g, s - LAG)

            group(0)
            with pe.Fori(1, G) as g:
                group(g)
            back(G)

        @block.scalar
        def _(act):
            chain = [0]

            def link(ins):
                chain[0] += 1
                ins.then_inc(act_chain, 1)
                act.wait_ge(act_chain, chain[0])

            def root(src, tmp, dst, ready):
                link(nc.scalar.activation(tmp, src, ACT.Ln))
                nc.scalar.activation(dst, tmp, ACT.Exp, scale=-0.5).then_inc(ready, 1)

            def split_hi(e):
                nc.scalar.activation(w_hi[:, e % WSPLIT, :], w_stage[:, e, HC:], ACT.Copy).then_inc(w_hi_ready, 1)

            act.preload_act_table_set("natural_log_exp_and_others")
            act.wait_ge(noise_ready, 1)
            root(noise_abs[:], noise_log[:], noise_log[:], noise_root)
            act.wait_ge(cap_ready, 1)
            nc.scalar.activation(gate_u[:], gate_cap[:], ACT.Exp).then_inc(u_ready, 1)
            for e in range(2):
                act.wait_ge(w_landed[e], 16)
                split_hi(e)
            act.wait_ge(var_ready, 1)
            root(small[:, 0, :], small[:, 1, :], small[:, 2, :], root_ready)
            act.wait_ge(xhatT_mm, 1)
            nc.scalar.activation(xhatT[:], bank[3][:], ACT.Copy).then_inc(xhatT_ready, 1)
            act.wait_ge(qk_ready, 1)
            for h in range(HEADS // 2, HEADS):
                nc.scalar.activation(k_heads[:, :, h, :], qkT[:, 1, :].rearrange("p (b l) -> p b l", b=IMG), ACT.Copy,
                                     scale=mid[:, MID_AT["headmask"].start + h:MID_AT["headmask"].start + h + 1]).then_inc(k_heads_act, 1)
            for c in range(NC):
                act.wait_ge(shifted_ready, c + 1)
                nc.scalar.activation(probs[:, c, :], shifted[:, c, :], ACT.Exp, scale=float(HD) ** -0.5).then_inc(probs_ready, 1)
            pt_bank = [6, 7, 0, 1]
            for c in range(NC):
                act.wait_ge(probsT_mm, c + 1)
                nc.scalar.activation(probsT[:, c, :], bank[pt_bank[c]][:], ACT.Copy).then_inc(probsT_ready, 1)
            act.wait_ge(attn_mm, 1)
            nc.scalar.activation(attnT[:], bank[2][:], ACT.Identity, bias=md("bv")).then_inc(attn_ready, 1)
            act.wait_ge(var_ready, 2)
            root(small[:, 0, :], small[:, 1, :], small[:, 2, :], root_ready)
            act.wait_ge(var_ready, 3)
            root(small[:, 4, :], small[:, 1, :], small[:, 5, :], root_ready)
            act.wait_ge(inpT_mm, 1)
            nc.scalar.activation(inpT[:], bank[4][:], ACT.Copy).then_inc(inpT_ready, 1)
            act.wait_ge(zT_ready, 1)
            nc.scalar.activation(z_hi[:], zT[:], ACT.Copy).then_inc(z_hi_ready, 1)
            act.wait_ge(gap_ready, 1)
            nc.scalar.activation(top[:, 5, :], top[:, 4, :], ACT.Exp).then_inc(gap_exp, 1)
            act.wait_ge(gatesT_mm, 1)
            nc.scalar.activation(gatesT[:], bank[7][0:SETS * E, :], ACT.Copy).then_inc(gatesT_ready, 1)

            def y_root(g):
                act.wait_ge(y_var_ready, g)
                if isinstance(g, int):
                    act.wait_ge(y_var_ready, g)
                nc.scalar.activation(y_small[:, 1, :], y_small[:, 0, :], ACT.Ln).then_inc(y_root_ready, 1)
                act.wait_ge(y_root_ready, 2 * g - 1)
                nc.scalar.activation(y_small[:, 2, :], y_small[:, 1, :], ACT.Exp, scale=-0.5).then_inc(y_root_ready, 1)

            def group(g):
                for s in range(STEPS):
                    e, c = divmod(s, HC)
                    if c == 1:
                        n = e + 2
                        act.wait_ge(w_landed[n % E], g * 16 + 16 * (1 + n // E))
                        if not (isinstance(g, int) and n < WSPLIT):
                            act.wait_ge(down_done, g * STEPS + HC * (n - WSPLIT + 1))
                        split_hi(n % E)
                    act.wait_ge(up_done, g * STEPS + (s + 1))
                    if not (isinstance(g, int) and s < HC):
                        act.wait_ge(split_done, g * STEPS + (s + 1 - HC))
                    nc.scalar.activation(relu[:, c, :], bank[c][:], ACT.Relu, bias=w_stage[:, e, c:c + 1]).then_inc(relu_done, 1)
                    if s == 4 * HC - 1 and not isinstance(g, int):
                        y_root(g)

            group(0)
            with act.Fori(1, G) as g:
                group(g)
            y_root(G)

        @block.gpsimd
        def _(pool):
            def split_lo(e):
                nc.gpsimd.tensor_tensor(w_lo[:, e % WSPLIT, :], w_stage[:, e, HC:], w_hi[:, e % WSPLIT, :], ALU.subtract).then_inc(w_lo_ready, 1)

            for e in range(2):
                pool.wait_ge(w_hi_ready, e + 1)
                split_lo(e)
            pool.wait_ge(mid_landed, 16)
            pool.wait_ge(h0_ready, 1)
            nc.gpsimd.tensor_tensor(h0_bproj[:], h0[:], md("bproj").unsqueeze(1).to_broadcast([P, NC, D]), ALU.add).then_inc(h0b_ready, 1)
            for c in range(NC):
                pool.wait_ge(inv_ready, c + 1)
                nc.gpsimd.tensor_tensor(probs_n[:, c, :].rearrange("p (h k) -> p h k", h=HEADS),
                                        probs[:, c, :].rearrange("p (h k) -> p h k", h=HEADS),
                                        wide(row_inv[:, c, :].unsqueeze(2), [P, HEADS, L]), ALU.mult).then_inc(probs_normed, 1)

            def group(g):
                for e in range(E):
                    n = e + 2
                    pool.wait_ge(w_hi_ready, g * E + (n + 1))
                    split_lo(n % E)
                    if isinstance(g, int) and e == 0:
                        pool.wait_ge(moe_seeded, G)
                    pool.wait_ge(o_gated_ready, g * E + (e + 1))
                    if not (isinstance(g, int) and e == 0):
                        pool.wait_ge(o_summed, g * E + e)
                    acc = moeT[:, g, :] if isinstance(g, int) else moeT[:, bass.ds(g, 1), :].rearrange("p a n -> p (a n)")
                    if e == E - 1 and not isinstance(g, int):
                        pool.wait_ge(yT_mm, g)
                    pool.sem_inc(held, 1)
                    nc.gpsimd.tensor_tensor(moe_sumT[:] if e == E - 1 else acc, acc, o_gated[:, e % 2, :], ALU.add).then_inc(o_summed, 1)

            group(0)
            with pool.Fori(1, G) as g:
                group(g)

        @block.vector
        def _(dve):
            chain = [0]

            def link(ins):
                chain[0] += 1
                ins.then_inc(dve_chain, 1)
                dve.wait_ge(dve_chain, chain[0])

            def newton(ve, y, t, out_):
                link(nc.vector.scalar_tensor_tensor(t, y, -0.5, y, ALU.mult, ALU.mult))
                link(nc.vector.tensor_tensor(t, t, ve, ALU.mult))
                link(nc.vector.scalar_tensor_tensor(out_, t, 1.5, y, ALU.add, ALU.mult))

            def token_stats(src):
                for c in range(NC):
                    ins = nc.vector.bn_stats(stats[:, c, :], src[:, c, :])
                link(ins)
                for c in range(NC):
                    ins = nc.vector.bn_aggr(mv[:, c, :], stats[:, c, :])
                link(ins)
                nc.vector.tensor_scalar(small[:, 0, :], mv[:, :, 1], EPS, None, ALU.add).then_inc(var_ready, 1)

            dve.wait_ge(tok_landed, 16)
            link(nc.vector.scalar_tensor_tensor(noise_abs[:], tok[:, 0:NOISE], -1.0, tok[:, 0:NOISE], ALU.mult, ALU.max))
            nc.vector.tensor_scalar(noise_abs[:], noise_abs[:], TINY, None, ALU.max).then_inc(noise_ready, 1)
            dve.wait_ge(noise_root, 1)
            link(nc.vector.tensor_tensor(noise_f[:], tok[:, 0:NOISE], noise_log[:], ALU.mult))
            f_in = noise_f[:, 0:KF * 2]
            f_out = noise_f[:, KF * 2:KF * 2 + 2]
            f_row = noise_f[:, KF * 2 + 2:NOISE]
            nc.vector.tensor_tensor(b_noisy[:], tk("sb"), f_out, ALU.mult).then_inc(dve_chain, 1)
            chain[0] += 1
            link(nc.vector.tensor_tensor(w_noise[:].rearrange("p (k n) -> p k n", k=KF), tk("sw").rearrange("p (k n) -> p k n", k=KF),
                                         f_row.unsqueeze(1).to_broadcast([P, KF, 2 * D]), ALU.mult))
            link(nc.vector.tensor_tensor(b_noisy[:], b_noisy[:], tk("b"), ALU.add))
            for i in range(KF * 2):
                cols = slice(i * D, (i + 1) * D)
                ins = nc.vector.scalar_tensor_tensor(w_noisy[:, cols], w_noise[:, cols], f_in[:, i:i + 1], tk("w")[:, cols], ALU.mult, ALU.add)
            ins.then_inc(weights_noisy, 1)
            dve.wait_ge(mid_landed, 16)
            link(nc.vector.tensor_tensor(pe_b3[:], md("pe"), md("b3"), ALU.add))
            dve.wait_ge(gate_mm, 1)
            nc.vector.tensor_scalar(gate_cap[:], bank[0][:], b_noisy[:, 0:1], 20.0, ALU.add, ALU.min).then_inc(cap_ready, 1)
            link(nc.vector.tensor_scalar(gate_in[:], bank[0][:], b_noisy[:, 0:1], None, ALU.add))
            dve.wait_ge(u_ready, 1)
            link(nc.vector.scalar_tensor_tensor(gate_n[:], gate_u[:], 2.0, gate_u[:], ALU.add, ALU.mult))
            link(nc.vector.tensor_scalar(gate_d[:], gate_n[:], 2.0, None, ALU.add))
            link(nc.vector.reciprocal(gate_r[:], gate_d[:]))
            link(nc.vector.tensor_tensor(gate_n[:], gate_n[:], gate_r[:], ALU.mult))
            link(nc.vector.tensor_tensor(gate_n[:], gate_n[:], gate_in[:], ALU.mult))
            dve.wait_ge(inner_mm, 1)
            nc.vector.scalar_tensor_tensor(gated[:], bank[1][:], b_noisy[:, 1:2], gate_n[:], ALU.add, ALU.mult).then_inc(gated_ready, 1)
            dve.wait_ge(h0_mm, 1)
            nc.vector.tensor_tensor(h0[:], bank[2][:].rearrange("p (c d) -> p c d", c=NC), pe_b3[:].unsqueeze(1).to_broadcast([P, NC, D]), ALU.add).then_inc(h0_ready, 1)
            dve.wait_ge(h0_ready, 1)
            token_stats(h0)
            dve.wait_ge(root_ready, 1)
            newton(small[:, 0, :], small[:, 2, :], small[:, 3, :], small[:, 6, :])
            for c in range(NC):
                nc.vector.tensor_scalar(xhat[:, c, :], h0[:, c, :], mv[:, c, 0:1], small[:, 6, c:c + 1], ALU.subtract, ALU.mult).then_inc(xhat_ready, 1)
            for n, (i, name, table) in enumerate([(1, "k", "cos"), (1, "ks", "sin"), (0, "q", "cos"), (0, "qs", "sin")]):
                src = {"q": 0, "qs": 1, "k": 2, "ks": 3}[name]
                dst = rot_a if table == "cos" else rot_b
                dve.wait_ge(qk_mm, src + 1)
                link(nc.vector.scalar_tensor_tensor(dst[:, i, :].rearrange("p (b l) -> p b l", b=IMG), bank[4 + src][:].rearrange("p (b l) -> p b l", b=IMG),
                                                    mid[:, MID_AT["bqkv"].start + src:MID_AT["bqkv"].start + src + 1],
                                                    md(table).unsqueeze(1).to_broadcast([P, IMG, L]), ALU.add, ALU.mult))
                if table == "sin":
                    nc.vector.tensor_tensor(qkT[:, i, :], rot_a[:, i, :], rot_b[:, i, :], ALU.add).then_inc(qk_ready, 1)
                if name == "ks":
                    dve.wait_ge(qk_ready, 1)
                    for h in range(HEADS // 2):
                        nc.vector.tensor_scalar(k_heads[:, :, h, :], qkT[:, 1, :].rearrange("p (b l) -> p b l", b=IMG),
                                                mid[:, MID_AT["headmask"].start + h:MID_AT["headmask"].start + h + 1], None, ALU.mult).then_inc(k_heads_dve, 1)
            for i in range(2):
                dve.wait_ge(v_mm, i + 1)
                nc.vector.tensor_tensor(v_heads[:, 4 * i:4 * i + 4, :], bank[i][:].rearrange("p (b d) -> p b d", b=4),
                                        md("parmask").unsqueeze(1).to_broadcast([P, 4, D]), ALU.mult).then_inc(v_ready, 1)
            def soft_sum(c):
                dve.wait_ge(probs_ready, c + 1)
                link(nc.vector.tensor_reduce(row_sum[:, c, :], probs[:, c, :].rearrange("p (h k) -> p h k", h=HEADS), AX.X, ALU.add))
                nc.vector.reciprocal(row_inv[:, c, :], row_sum[:, c, :]).then_inc(inv_ready, 1)

            for c in range(NC):
                dve.wait_ge(scores_mm, c + 1)
                s3 = bank[2 + c][:].rearrange("p (h k) -> p h k", h=HEADS)
                link(nc.vector.tensor_reduce(row_max[:, c, :], s3, AX.X, ALU.max))
                nc.vector.tensor_tensor(shifted[:, c, :].rearrange("p (h k) -> p h k", h=HEADS), s3,
                                        wide(row_max[:, c, :].unsqueeze(2), [P, HEADS, L]), ALU.subtract).then_inc(shifted_ready, 1)
                if c >= 1:
                    soft_sum(c - 1)
            soft_sum(NC - 1)
            dve.wait_ge(proj_mm, 1)
            dve.wait_ge(h0b_ready, 1)
            link(nc.vector.tensor_tensor(h1[:], bank[3][:].rearrange("p (c d) -> p c d", c=NC), h0_bproj[:], ALU.add))
            token_stats(h1)
            dve.wait_ge(root_ready, 2)
            newton(small[:, 0, :], small[:, 2, :], small[:, 3, :], small[:, 6, :])
            for c in range(NC):
                nc.vector.tensor_scalar(inp[:, c, :], h1[:, c, :], mv[:, c, 0:1], small[:, 6, c:c + 1], ALU.subtract, ALU.mult).then_inc(inp_ready, 1)
            link(nc.vector.tensor_tensor(small[:, 7, :], small[:, 6, :], small[:, 6, :], ALU.mult))
            link(nc.vector.tensor_tensor(small[:, 7, :], small[:, 7, :], mv[:, :, 1], ALU.mult))
            nc.vector.tensor_scalar(small[:, 4, :], small[:, 7, :], EPS, None, ALU.add).then_inc(var_ready, 1)
            dve.wait_ge(root_ready, 3)
            newton(small[:, 4, :], small[:, 5, :], small[:, 3, :], small[:, 7, :])
            dve.wait_ge(inp_ready, NC)
            for c in range(NC):
                nc.vector.tensor_scalar(zhat[:, c, :], inp[:, c, :], small[:, 7, c:c + 1], None, ALU.mult).then_inc(zhat_ready, 1)
            dve.wait_ge(ffn_landed, 16)
            dve.wait_ge(zT_mm, 1)
            nc.vector.tensor_scalar(zT[:], bank[5][:], ff("ln_g"), ff("ln_b"), ALU.mult, ALU.add).then_inc(zT_ready, 1)
            nc.vector.tensor_tensor(out_acc[:], h1[:], inp[:], ALU.add).then_inc(dve_chain, 1)
            chain[0] += 1
            dve.wait_ge(z_hi_ready, 1)
            nc.vector.tensor_tensor(z_lo[:], zT[:], z_hi[:], ALU.subtract).then_inc(z_lo_ready, 1)
            flat = lambda t: t[:].rearrange("p c s e -> p (c s) e")
            spread = lambda ap: ap.unsqueeze(2).to_broadcast([P, NC * SETS, E])
            order = ff("order").unsqueeze(1).to_broadcast([P, NC * SETS, E])
            nc.vector.memset(logits[:, :, G, G:E], -1e30).then_inc(dve_chain, 1)
            dve.wait_ge(logits_mm, 1)
            nc.vector.tensor_copy(logits[:, :, G, 0:G], bank[6][:, 0:NC * G].rearrange("p (c g) -> p c g", c=NC)).then_inc(dve_chain, 1)
            chain[0] += 2
            for c in range(NC):
                ins = nc.vector.tensor_copy(logits[:, c, 0:G, :], bank[6][:, 128 + c * G * E:128 + (c + 1) * G * E].rearrange("p (g e) -> p g e", g=G))
            link(ins)
            link(nc.vector.tensor_reduce(top[:, 0, :], flat(logits), AX.X, ALU.max))
            link(nc.vector.tensor_tensor(flat(equal), flat(logits), spread(top[:, 0, :]), ALU.is_equal))
            link(nc.vector.tensor_tensor(flat(key), flat(equal), order, ALU.mult))
            link(nc.vector.tensor_reduce(top[:, 1, :], flat(key), AX.X, ALU.max))
            link(nc.vector.tensor_tensor(flat(first), flat(key), spread(top[:, 1, :]), ALU.is_equal))
            link(nc.vector.scalar_tensor_tensor(flat(rest), flat(first), -1e38, flat(logits), ALU.mult, ALU.add))
            link(nc.vector.tensor_reduce(top[:, 2, :], flat(rest), AX.X, ALU.max))
            nc.vector.tensor_tensor(top[:, 4, :], top[:, 2, :], top[:, 0, :], ALU.subtract).then_inc(gap_ready, 1)
            link(nc.vector.tensor_tensor(flat(equal), flat(rest), spread(top[:, 2, :]), ALU.is_equal))
            link(nc.vector.tensor_tensor(flat(key), flat(equal), order, ALU.mult))
            link(nc.vector.tensor_reduce(top[:, 3, :], flat(key), AX.X, ALU.max))
            link(nc.vector.tensor_tensor(flat(second), flat(key), spread(top[:, 3, :]), ALU.is_equal))
            dve.wait_ge(gap_exp, 1)
            link(nc.vector.tensor_scalar(top[:, 6, :], top[:, 5, :], 1.0, None, ALU.add))
            link(nc.vector.reciprocal(top[:, 7, :], top[:, 6, :]))
            link(nc.vector.tensor_tensor(top[:, 6, :], top[:, 5, :], top[:, 7, :], ALU.mult))
            link(nc.vector.tensor_tensor(flat(first), flat(first), spread(top[:, 7, :]), ALU.mult))
            link(nc.vector.tensor_tensor(flat(second), flat(second), spread(top[:, 6, :]), ALU.mult))
            nc.vector.tensor_tensor(flat(gates), flat(first), flat(second), ALU.add).then_inc(gates_ready, 1)

            def seed():
                for g in range(G):
                    dve.wait_ge(b2_mm, g + 1)
                    nc.vector.tensor_tensor(moeT[:, g, :], bank[6 + g % 2][:], zT[:], ALU.add).then_inc(moe_seeded, 1)
                dve.wait_ge(seed_out_mm, 1)
                link(nc.vector.tensor_tensor(out_acc[:], bank[7][:].rearrange("p (c d) -> p c d", c=NC), out_acc[:], ALU.add))

            def split(g, s):
                e, c = divmod(s, HC)
                dve.wait_ge(relu_done, g * STEPS + (s + 1))
                if not (isinstance(g, int) and s < 2 * HC):
                    dve.wait_ge(down_done, g * STEPS + (s + 1 - 2 * HC))
                nc.vector.tensor_copy(h_hi[:, e % 2, c, :], relu[:, c, :]).then_inc(hi_done, 1)
                dve.wait_ge(hi_done, g * STEPS + (s + 1))
                nc.vector.tensor_tensor(h_lo[:, e % 2, c, :], relu[:, c, :], h_hi[:, e % 2, c, :], ALU.subtract).then_inc(split_done, 1)

            def gate_output(g, e):
                dve.wait_ge(down_done, g * STEPS + HC * (e + 1))
                dve.wait_ge(iw_landed[e], g * 16 + 16)
                if not (isinstance(g, int) and e < 2):
                    dve.wait_ge(o_summed, g * E + (e - 1))
                nc.vector.tensor_tensor(o_gated[:, e % 2, :], bank[4 + e % 2][:], iw_rows[:, e, :], ALU.mult).then_inc(o_gated_ready, 1)

            y3 = bank[6][:].rearrange("p (c d) -> p c d", c=NC)
            YLINKS = 9

            def y_link(ins, g, n):
                ins.then_inc(yT_read, 1)
                dve.wait_ge(yT_read, g * YLINKS + (n + 1 - YLINKS))

            def y_var(g):
                dve.wait_ge(yT_mm, g)
                for c in range(NC):
                    ins = nc.vector.bn_stats(y_stats[:, c, :], y3[:, c, :])
                y_link(ins, g, 0)
                dve.sem_inc(held, 1)
                for c in range(NC):
                    ins = nc.vector.bn_aggr(y_mv[:, c, :], y_stats[:, c, :])
                y_link(ins, g, 1)
                nc.vector.tensor_scalar(y_small[:, 0, :], y_mv[:, :, 1], EPS, None, ALU.add).then_inc(y_var_ready, 1)

            def y_out(g):
                dve.wait_ge(y_root_ready, 2 * g)
                y = y_small[:, 2, :]
                y_link(nc.vector.scalar_tensor_tensor(y_small[:, 3, :], y, -0.5, y, ALU.mult, ALU.mult), g, 2)
                y_link(nc.vector.tensor_tensor(y_small[:, 3, :], y_small[:, 3, :], y_small[:, 0, :], ALU.mult), g, 3)
                y_link(nc.vector.scalar_tensor_tensor(y_small[:, 4, :], y_small[:, 3, :], 1.5, y, ALU.add, ALU.mult), g, 4)
                if isinstance(g, int):
                    gw = gates[:, :, G, g - 1]
                    gain = ffn[:, FFN_AT["gln_g"].start + (g - 1) * D:FFN_AT["gln_g"].start + g * D].unsqueeze(1)
                else:
                    gw = gates[:, :, G, bass.ds(g - 1, 1)].rearrange("p c a -> p (c a)")
                    gain = ff("gln_g").rearrange("p (g d) -> p g d", g=G)[:, bass.ds(g - 1, 1), :]
                y_link(nc.vector.tensor_tensor(y_small[:, 5, :], y_small[:, 4, :], gw, ALU.mult), g, 5)
                for c in range(NC):
                    ins = nc.vector.tensor_scalar(y_hat[:, c, :], y3[:, c, :], y_mv[:, c, 0:1], y_small[:, 5, c:c + 1], ALU.subtract, ALU.mult)
                y_link(ins, g, 6)
                y_link(nc.vector.tensor_tensor(y_scaled[:], y_hat[:], gain.to_broadcast([P, NC, D]), ALU.mult), g, 7)
                y_link(nc.vector.tensor_tensor(out_acc[:], out_acc[:], y_scaled[:], ALU.add), g, 8)

            def group(g):
                for s in range(STEPS):
                    split(g, s)
                    if s % HC == HC - 1 and s >= 2 * HC - 1:
                        gate_output(g, s // HC - 1)
                    if not isinstance(g, int):
                        if s == 2 * HC + 2:
                            y_var(g)
                        if s == 4 * HC + 1:
                            y_out(g)
                gate_output(g, E - 1)

            seed()
            group(0)
            with dve.Fori(1, G) as g:
                group(g)
            y_var(G)
            y_out(G)
            nc.vector.engine_nop().then_inc(out_ready, 1)


def shape_tables():
    pos = np.arange(L, dtype=np.float32)[:, None]
    div = np.exp(np.arange(0, D, 2, dtype=np.float32) * np.float32(-np.log(10000.0) / D)).astype(np.float32)
    ang = (pos * div).astype(np.float32)
    pe = np.stack([np.sin(ang), np.cos(ang)], axis=-1).reshape(L, D).astype(np.float32)
    freqs = (1.0 / np.float32(10000.0) ** (np.arange(0, HD, 2, dtype=np.float32) / HD)).astype(np.float32)
    turn = np.outer(np.arange(L, dtype=np.float32), freqs).astype(np.float32)
    dim = np.arange(D) % HD
    cos = np.cos(turn)[:, dim // 2].T.astype(np.float32)
    sin = (np.sin(turn)[:, dim // 2].T * np.where(dim % 2 == 0, -1.0, 1.0)[:, None]).astype(np.float32)
    p = np.arange(P)
    headmask = (p[:, None] // HD == np.arange(HEADS)[None, :]).astype(np.float32)
    parmask = (p[:, None] // L == (np.arange(D)[None, :] // HD) % 2).astype(np.float32)
    order = np.tile(np.arange(E, 0, -1, dtype=np.float32), (P, 1))
    return {"pe": np.concatenate([pe] * (P // L)), "cos": cos, "sin": sin, "headmask": headmask,
            "parmask": parmask, "order": order, "ident": np.eye(P, dtype=np.float32)}


def kernel(**inputs):
    import concourse.bacc as bacc
    from concourse.bass_utils import run_bass_kernel_spmd

    a = {k: np.asarray(v) for k, v in inputs.items()}
    t = shape_tables()

    def rows(v):
        return np.broadcast_to(v.reshape(1, -1), (P, v.size))

    def pack(parts, values):
        return np.ascontiguousarray(np.concatenate([values[n].reshape(P, w) for n, w in parts], axis=1))

    def feat(wa, wb):
        return np.stack([wa, wb]).reshape(2, D, KF, P).transpose(3, 2, 0, 1)

    x = a["x"].reshape(IMG, SIDE, PATCH, SIDE, PATCH).transpose(2, 4, 0, 1, 3).reshape(KF, P, N).transpose(1, 0, 2)
    tok = {
        "noise_in": np.stack([a["L0_tok_eps_in1"], a["L0_tok_eps_in2"]]).reshape(2, KF, P).transpose(2, 1, 0),
        "noise_out": np.stack([a["L0_tok_eps_out1"], a["L0_tok_eps_out2"]], axis=1),
        "noise_row": rows(np.stack([a["L0_tok_eps_out1"], a["L0_tok_eps_out2"]])),
        "b": np.stack([a["L0_tok_W1_b"], a["L0_tok_W2_b"]], axis=1),
        "sb": np.stack([a["L0_tok_W1_sb"], a["L0_tok_W2_sb"]], axis=1),
        "w": feat(a["L0_tok_W1_w"], a["L0_tok_W2_w"]),
        "sw": feat(a["L0_tok_W1_sw"], a["L0_tok_W2_sw"]),
        "xT": x,
    }
    swap = np.arange(D) ^ 1
    wq, wk, wv = a["L0_attn_Wqkv"].reshape(3, D, D)
    bq, bk, bv = a["L0_attn_bqkv"].reshape(3, D)
    mid = {
        "w3T": a["L0_tok_W3_w"].T, "b3": rows(a["L0_tok_W3_b"]), "pe": t["pe"], "ident": t["ident"],
        "wqkvT": np.concatenate([wq.T, wq[swap].T, wk.T, wk[swap].T, wv.T], axis=1),
        "bqkv": np.stack([bq, bq[swap], bk, bk[swap]], axis=1), "bv": bv,
        "cos": t["cos"], "sin": t["sin"], "headmask": t["headmask"], "parmask": t["parmask"],
        "wprojT": a["L0_attn_Wproj"].T, "bproj": rows(a["L0_attn_bproj"]),
    }
    b2 = np.zeros((P, G, D), np.float32)
    for g in range(G):
        b2[g * E:(g + 1) * E, g] = a["L0_ffn_b2"][g]
    gln_b = np.zeros((P, D), np.float32)
    gln_b[G * E:G * E + G] = a["L0_ffn_gln_b"]
    ffn = {
        "wg": a["L0_ffn_wg_group"], "wgi": a["L0_ffn_wg_inner"].transpose(1, 0, 2), "ln_g": a["L0_ffn_ln_g"],
        "ln_b": a["L0_ffn_ln_b"], "order": t["order"], "gln_g": rows(a["L0_ffn_gln_g"]), "gln_b": gln_b, "b2": b2,
    }
    experts = np.concatenate([
        a["L0_ffn_b1"].reshape(G * E, HC, P).transpose(0, 2, 1),
        a["L0_ffn_W1"].reshape(G * E, D, H),
        a["L0_ffn_W2"].reshape(G * E, HC, P, D).transpose(0, 2, 1, 3).reshape(G * E, P, H)], axis=2)
    arrays = {"tok_in": pack(TOK_PARTS, tok), "mid_in": pack(MID_PARTS, mid), "ffn_in": pack(FFN_PARTS, ffn),
              "experts_in": np.ascontiguousarray(experts)}

    nc = bacc.Bacc("TRN2", target_bir_lowering=False, num_devices=1)
    args = [nc.dram_tensor(n, v.shape, F32, kind="ExternalInput").ap() for n, v in arrays.items()]
    out = nc.dram_tensor("out", (N, D), F32, kind="ExternalOutput").ap()
    vit_tower(nc, *args, out)
    r = run_bass_kernel_spmd(nc, [arrays], core_ids=[0])
    return r.results[0]["out"].reshape(IMG, L, D)
```

```python
from contextlib import ExitStack

import numpy as np

import concourse.bass as bass
from concourse import mybir

F32 = mybir.dt.float32
F16 = mybir.dt.float16
ALU = mybir.AluOpType
ACT = mybir.ActivationFunctionType
AX = mybir.AxisListType

P = 128
IMG, PIX, PATCH = 8, 128, 16
SIDE = PIX // PATCH
L = SIDE * SIDE
N = IMG * L
NC = N // P
FEAT = PATCH * PATCH
KF = FEAT // P
D = 128
HEADS = 8
HD = D // HEADS
G, E, H = 4, 8, 512
HC = H // P
SETS = G + 1
EPS = 1e-5
TINY = 2.0 ** -60
WCOLS = HC + 2 * H
WSPLIT = 4
AHEAD = 2
STEPS = E * HC
LAG = 6
OUT_LAG = 2
RING = 8
ACT_HIGH = (0, 2)
BACK_STEP = 9
Y_ROOT_STEP = 18
DVE_HEADS = 5
SEED_STEP = LAG + 2
PT_BANK = [6, 7, 0, 1]


def columns(parts):
    at, where = 0, {}
    for name, width in parts:
        where[name] = slice(at, at + width)
        at += width
    return where, at


TOK_PARTS = [("noise_in", KF * 2), ("noise_out", 2), ("noise_row", 2 * D), ("b", 2), ("sb", 2), ("w", KF * 2 * D),
             ("sw", KF * 2 * D)]
MID_PARTS = [("w3T", D), ("b3", D), ("pe", D), ("ident", D), ("wqkvT", 5 * D), ("bqkv", 4), ("bv", 1),
             ("cos", L), ("sin", L), ("headmask", HEADS), ("parmask", D), ("wprojT", D), ("bproj", D)]
FFN_PARTS = [("wg", G), ("wgi", G * E), ("ln_g", 1), ("ln_b", 1), ("order", E), ("gln_g", G * D), ("gln_b", D),
             ("b2", G * D)]
TOK_AT, TOK_W = columns(TOK_PARTS)
MID_AT, MID_W = columns(MID_PARTS)
FFN_AT, FFN_W = columns(FFN_PARTS)


def vit_tower(nc, tok_in, x_in, mid_in, ffn_in, experts, out):
    ctx = ExitStack()
    with ctx:
        def sb(name, shape, dt=F32):
            return ctx.enter_context(nc.sbuf_tensor(name, shape, dt))

        def sem(name):
            return ctx.enter_context(nc.semaphore(name))

        bank = [ctx.enter_context(nc.psum_tensor(f"bank{i}", [P, 512], F32)) for i in range(8)]
        gates_dram = nc.dram_tensor("gates_t", [G * E, N], F32)

        tok = sb("tok", [P, TOK_W])
        patches = sb("patches", [P, KF, N])
        mid = sb("mid", [P, MID_W])
        ffn = sb("ffn", [P, FFN_W])

        def tk(name):
            return tok[:, TOK_AT[name]]

        def md(name):
            return mid[:, MID_AT[name]]

        def ff(name):
            return ffn[:, FFN_AT[name]]

        NOISE = KF * 2 + 2 + 2 * D
        noise_abs = sb("noise_abs", [P, NOISE])
        noise_log = sb("noise_log", [P, NOISE])
        noise_f = sb("noise_f", [P, NOISE])
        w_noise = sb("w_noise", [P, KF * 2 * D])
        w_noisy = sb("w_noisy", [P, KF * 2 * D])
        b_noisy = sb("b_noisy", [P, 2])
        gate_in = sb("gate_in", [P, N])
        gate_cap = sb("gate_cap", [P, N])
        gate_u = sb("gate_u", [P, N])
        gate_n = sb("gate_n", [P, N])
        gate_d = sb("gate_d", [P, N])
        gate_r = sb("gate_r", [P, N])
        gated = sb("gated", [P, N])
        pe_b3 = sb("pe_b3", [P, D])
        h0 = sb("h0", [P, NC, D])
        h0_bproj = sb("h0_bproj", [P, NC, D])
        stats = sb("stats", [P, NC, 6])
        mv = sb("mv", [P, NC, 2])
        small = sb("small", [P, 8, NC])
        xhat = sb("xhat", [P, NC, D])
        xhatT = sb("xhatT", [P, N])
        rot_a = sb("rot_a", [P, 2, N])
        rot_b = sb("rot_b", [P, 2, N])
        qkT = sb("qkT", [P, 2, N])
        k_heads = sb("k_heads", [P, IMG, HEADS, L])
        v_heads = sb("v_heads", [P, IMG, D])
        row_max = sb("row_max", [P, NC, HEADS])
        row_sum = sb("row_sum", [P, NC, HEADS])
        row_inv = sb("row_inv", [P, NC, HEADS])
        shifted = sb("shifted", [P, NC, HEADS * L])
        probs_both = sb("probs_both", [P, 2, NC, HEADS * L])
        probs, probsT = probs_both[:, 0], probs_both[:, 1]
        probs_n = sb("probs_n", [P, NC, HEADS * L])
        attnT = sb("attnT", [P, N])
        h1 = sb("h1", [P, NC, D])
        inp = sb("inp", [P, NC, D])
        zhat = sb("zhat", [P, NC, D])
        inpT = sb("inpT", [P, N])
        zT = sb("zT", [P, N])
        z_hi = sb("z_hi", [P, N], F16)
        z_lo = sb("z_lo", [P, N], F16)
        logits = sb("logits", [P, NC, SETS, E])
        rest = sb("rest", [P, NC, SETS, E])
        equal = sb("equal", [P, NC, SETS, E])
        key = sb("key", [P, NC, SETS, E])
        first = sb("first", [P, NC, SETS, E])
        second = sb("second", [P, NC, SETS, E])
        gates = sb("gates", [P, NC, SETS, E])
        top = sb("top", [P, 8, NC * SETS])
        gatesT = sb("gatesT", [SETS * E, N])
        out_acc = sb("out_acc", [P, NC, D])

        w_stage = sb("w_stage", [P, E, WCOLS])
        w_hi = sb("w_hi", [P, WSPLIT, 2 * H], F16)
        w_lo = sb("w_lo", [P, WSPLIT, 2 * H], F16)
        iw_rows = k_heads[:].rearrange("p b h k -> p (b h k)").rearrange("p (e n) -> p e n", e=E)
        relu = probs_both[:].rearrange("p t c n -> p (t c) n")
        h_hi = shifted[:].rearrange("p c n -> p (c n)").bitcast(F16).rearrange("p (t c n) -> p t c n", t=2, c=HC)
        h_lo = probs_n[:].rearrange("p c n -> p (c n)").bitcast(F16).rearrange("p (t c n) -> p t c n", t=2, c=HC)
        o_gated = sb("o_gated", [P, 2, N])
        moeT = sb("moeT", [P, G, N])
        moe_sumT = sb("moe_sumT", [P, N])
        y_stats = sb("y_stats", [P, NC, 6])
        y_mv = sb("y_mv", [P, NC, 2])
        y_small = sb("y_small", [P, 6, NC])
        y_hat = sb("y_hat", [P, NC, D])
        y_scaled = sb("y_scaled", [P, NC, D])

        x_landed = sem("x_landed")
        tok_landed, mid_landed, ffn_landed = sem("tok_landed"), sem("mid_landed"), sem("ffn_landed")
        w_landed = [sem(f"w_landed{i}") for i in range(E)]
        iw_landed = [sem(f"iw_landed{i}") for i in range(E)]
        gates_stored, out_stored = sem("gates_stored"), sem("out_stored")
        dve_chain, act_chain, pool_chain = sem("dve_chain"), sem("act_chain"), sem("pool_chain")
        noise_ready, noise_root = sem("noise_ready"), sem("noise_root")
        weights_noisy = sem("weights_noisy")
        gate_mm, inner_mm = sem("gate_mm"), sem("inner_mm")
        cap_ready, u_ready = sem("cap_ready"), sem("u_ready")
        denom_ready, denom_inverse = sem("denom_ready"), sem("denom_inverse")
        gated_ready, h0_mm, h0_ready = sem("gated_ready"), sem("h0_mm"), sem("h0_ready")
        h0b_ready = sem("h0b_ready")
        var_ready, root_ready = sem("var_ready"), sem("root_ready")
        xhat_ready, xhatT_mm, xhatT_ready = sem("xhat_ready"), sem("xhatT_mm"), sem("xhatT_ready")
        qk_mm, v_mm = sem("qk_mm"), sem("v_mm")
        rot_ready, q_ready, k_ready = sem("rot_ready"), sem("q_ready"), sem("k_ready")
        k_heads_dve, k_heads_act, v_ready = sem("k_heads_dve"), sem("k_heads_act"), sem("v_ready")
        scores_mm, shifted_ready, probs_ready = sem("scores_mm"), sem("shifted_ready"), sem("probs_ready")
        inv_ready, probs_normed = sem("inv_ready"), sem("probs_normed")
        last_probs_normed = sem("last_probs_normed")
        probsT_mm, probsT_ready = sem("probsT_mm"), sem("probsT_ready")
        attn_mm, attn_ready, proj_mm = sem("attn_mm"), sem("attn_ready"), sem("proj_mm")
        shift_ready, out_seeded = sem("shift_ready"), sem("out_seeded")
        inp_ready, inpT_mm, inpT_ready = sem("inp_ready"), sem("inpT_mm"), sem("inpT_ready")
        zhat_ready, zT_mm, zT_ready = sem("zhat_ready"), sem("zT_mm"), sem("zT_ready")
        z_hi_ready, z_lo_ready = sem("z_hi_ready"), sem("z_lo_ready")
        logits_mm, gap_ready, gap_exp = sem("logits_mm"), sem("gap_ready"), sem("gap_exp")
        gates_ready, gatesT_mm, gatesT_ready = sem("gates_ready"), sem("gatesT_mm"), sem("gatesT_ready")
        b2_mm, moe_seeded, seed_out_mm = sem("b2_mm"), sem("moe_seeded"), sem("seed_out_mm")
        w_hi_ready, w_lo_ready = sem("w_hi_ready"), sem("w_lo_ready")
        up_done, relu_done = sem("up_done"), sem("relu_done")
        act_hi_done = sem("act_hi_done")
        hi_done, split_done, down_done = sem("hi_done"), sem("split_done"), sem("down_done")
        o_gated_ready, o_summed = sem("o_gated_ready"), sem("o_summed")
        yT_mm, y_var_ready, y_root_ready, yT_read = sem("yT_mm"), sem("y_var_ready"), sem("y_root_ready"), sem("yT_read")
        out_ready = sem("out_ready")
        held = sem("held")

        ident = md("ident")

        block = ctx.enter_context(nc.Block())

        def wide(ap, shape):
            return ap.to_broadcast(shape)

        def reuse(eng, signal, count):
            if not isinstance(count, int) or count > 0:
                eng.wait_ge(signal, count)

        @block.sync
        def _(sync):
            sync.dma_start(tok[:], tok_in).then_inc(tok_landed, 16)
            sync.dma_start(patches[:], x_in).then_inc(x_landed, 16)
            sync.dma_start(mid[:], mid_in).then_inc(mid_landed, 16)
            sync.dma_start(w_stage[:, 0, :], experts[0]).then_inc(w_landed[0], 16)
            sync.dma_start(ffn[:], ffn_in).then_inc(ffn_landed, 16)
            for e in range(1, E):
                sync.dma_start(w_stage[:, e, :], experts[e]).then_inc(w_landed[e], 16)
            sync.wait_ge(gatesT_ready, 1)
            sync.dma_start(gates_dram[:, :], gatesT[0:G * E, :]).then_inc(gates_stored, 16)
            sync.wait_ge(gates_stored, 16)
            for e in range(E):
                sync.dma_start(iw_rows[:, e, :], gates_dram[e:e + 1, :].to_broadcast([P, N])).then_inc(iw_landed[e], 16)
            with sync.Fori(1, G) as g:
                for e in range(E):
                    expert = sync.snap(g * E + e)
                    through, biased = sync.snap(g * E + (e + 1 - E)), sync.snap(g * STEPS + (HC * (e + 1) - STEPS))
                    sync.wait_ge(relu_done, biased)
                    sync.sem_inc(held, 1)
                    sync.dma_start(w_stage[:, e, :], experts[bass.ds(expert, 1), :, :].squeeze(0)).then_inc(w_landed[e], 16)
                    sync.wait_ge(o_gated_ready, through)
                    sync.sem_inc(held, 1)
                    sync.dma_start(iw_rows[:, e, :], gates_dram[bass.ds(expert, 1), :].to_broadcast([P, N])).then_inc(iw_landed[e], 16)
            for e in range(AHEAD):
                sync.wait_ge(w_lo_ready, (G - 1) * E + e + 1)
                sync.wait_ge(relu_done, (G - 1) * STEPS + HC * (e + 1))
                sync.dma_start(w_stage[:, e, 0:HC], experts[e, :, 0:HC]).then_inc(w_landed[e], 16)
            sync.wait_ge(out_ready, 1)
            sync.dma_start(out.rearrange("(c p) d -> p c d", p=P), out_acc[:]).then_inc(out_stored, 16)
            sync.wait_ge(out_stored, 16)

        @block.tensor
        def _(pe):
            pe.wait_ge(x_landed, 16)
            pe.wait_ge(weights_noisy, 1)
            wn = w_noisy[:].rearrange("p (k w h) -> p k w h", k=KF, w=2)
            for w, done in ((0, gate_mm), (1, inner_mm)):
                for k in range(KF):
                    mm = nc.tensor.matmul(bank[w][:], wn[:, k, w, :], patches[:, k, :], start=(k == 0), stop=(k == KF - 1))
                mm.then_inc(done, 1)
            pe.wait_ge(mid_landed, 16)
            pe.wait_ge(gated_ready, 1)
            for c in range(NC):
                mm = nc.tensor.matmul(bank[2][:, c * P:(c + 1) * P], gated[:, c * P:(c + 1) * P], md("w3T"), start=True, stop=True)
            mm.then_inc(h0_mm, 1)
            for c in range(NC):
                pe.wait_ge(xhat_ready, c + 1)
                mm = nc.tensor.transpose(bank[3][:, c * P:(c + 1) * P], xhat[:, c, :], ident)
            mm.then_inc(xhatT_mm, 1)
            pe.wait_ge(xhatT_ready, 1)
            for i in range(4):
                w = mid[:, MID_AT["wqkvT"].start + i * D:MID_AT["wqkvT"].start + (i + 1) * D]
                nc.tensor.matmul(bank[4 + i][:], w, xhatT[:], start=True, stop=True).then_inc(qk_mm, 1)
            wv = mid[:, MID_AT["wqkvT"].start + 4 * D:MID_AT["wqkvT"].start + 5 * D]
            for b in range(IMG):
                for half in range(2):
                    mm = nc.tensor.matmul(bank[b // 4][half * L:(half + 1) * L, (b % 4) * D:(b % 4 + 1) * D],
                                          xhatT[:, b * L:(b + 1) * L], wv, start=True, stop=True)
                if b % 4 == 3:
                    mm.then_inc(v_mm, 1)
            pe.wait_ge(q_ready, 1)
            pe.wait_ge(k_heads_dve, DVE_HEADS)
            pe.wait_ge(k_heads_act, HEADS - DVE_HEADS)
            pe.wait_ge(h0_ready, 1)
            for c in range(NC):
                for half in range(2):
                    b = 2 * c + half
                    mm = nc.tensor.matmul(bank[2 + c][half * L:(half + 1) * L, :], qkT[:, 0, b * L:(b + 1) * L],
                                          k_heads[:, b].rearrange("p h k -> p (h k)"), start=True, stop=True)
                mm.then_inc(scores_mm, 1)
            pe.wait_ge(v_ready, 2)
            for c in range(NC + 1):
                if c < NC:
                    pe.wait_ge(probs_normed if c < NC - 1 else last_probs_normed, c + 1 if c < NC - 1 else 1)
                    for hp in range(4):
                        mm = nc.tensor.transpose(bank[PT_BANK[c]][:, hp * P:(hp + 1) * P], probs_n[:, c, hp * P:(hp + 1) * P], ident)
                    mm.then_inc(probsT_mm, 1)
                if c >= 1:
                    pe.wait_ge(probsT_ready, c)
                    for half in range(2):
                        b = 2 * (c - 1) + half
                        for hp in range(4):
                            mm = nc.tensor.matmul(bank[2][hp * 32:(hp + 1) * 32, b * L:(b + 1) * L],
                                                  v_heads[:, b, hp * 32:(hp + 1) * 32],
                                                  probsT[:, c - 1, hp * P + half * L:hp * P + (half + 1) * L], start=True, stop=True)
            mm.then_inc(attn_mm, 1)
            pe.wait_ge(attn_ready, 1)
            for c in range(NC):
                mm = nc.tensor.matmul(bank[3][:, c * P:(c + 1) * P], attnT[:, c * P:(c + 1) * P], md("wprojT"), start=True, stop=True)
            mm.then_inc(proj_mm, 1)
            for c in range(NC):
                pe.wait_ge(zhat_ready, c + 1)
                mm = nc.tensor.transpose(bank[5][:, c * P:(c + 1) * P], zhat[:, c, :], ident)
            mm.then_inc(zT_mm, 1)
            for c in range(NC):
                pe.wait_ge(inp_ready, c + 1)
                mm = nc.tensor.transpose(bank[4][:, c * P:(c + 1) * P], inp[:, c, :], ident)
            mm.then_inc(inpT_mm, 1)
            pe.wait_ge(ffn_landed, 16)
            pe.wait_ge(inpT_ready, 1)
            for c in range(NC):
                nc.tensor.matmul(bank[6][:, c * G:(c + 1) * G], inpT[:, c * P:(c + 1) * P], ff("wg"), start=True, stop=True)
            pe.wait_ge(zT_ready, 1)
            for c in range(NC):
                mm = nc.tensor.matmul(bank[6][:, 128 + c * G * E:128 + (c + 1) * G * E], zT[:, c * P:(c + 1) * P], ff("wgi"), start=True, stop=True)
            mm.then_inc(logits_mm, 1)

            def up(g, s):
                e, c = divmod(s, HC)
                if c == 0:
                    pe.wait_ge(w_hi_ready, g * E + (e + 1))
                    pe.wait_ge(w_lo_ready, g * E + (e + 1))
                reuse(pe, relu_done, g * STEPS + (s + 1 - HC))
                cols = slice(c * P, (c + 1) * P)
                nc.tensor.matmul(bank[c][:], w_hi[:, e % WSPLIT, cols], z_hi[:], start=True, stop=False)
                nc.tensor.matmul(bank[c][:], w_hi[:, e % WSPLIT, cols], z_lo[:], start=False, stop=False)
                nc.tensor.matmul(bank[c][:], w_lo[:, e % WSPLIT, cols], z_hi[:], start=False, stop=True).then_inc(up_done, 1)

            def down(g, s):
                e, c = divmod(s, HC)
                pe.wait_ge(split_done, g * STEPS + (s + 1))
                if c == 0:
                    reuse(pe, o_gated_ready, g * E + (e - 1))
                cols = slice(H + c * D, H + (c + 1) * D)
                o = bank[4 + e % 2]
                nc.tensor.matmul(o[:], w_hi[:, e % WSPLIT, cols], h_hi[:, e % 2, c, :], start=(c == 0), stop=False)
                nc.tensor.matmul(o[:], w_hi[:, e % WSPLIT, cols], h_lo[:, e % 2, c, :], start=False, stop=False)
                nc.tensor.matmul(o[:], w_lo[:, e % WSPLIT, cols], h_hi[:, e % 2, c, :], start=False, stop=(c == HC - 1)).then_inc(down_done, 1)

            def back(g):
                pe.wait_ge(o_summed, g * E)
                for c in range(NC):
                    mm = nc.tensor.transpose(bank[6][:, c * P:(c + 1) * P],
                                             moe_sumT[:, c * P:(c + 1) * P], ident)
                mm.then_inc(yT_mm, 1)

            def gates_turn():
                pe.wait_ge(gates_ready, 1)
                for c in range(NC):
                    mm = nc.tensor.transpose(bank[7][0:SETS * E, c * P:(c + 1) * P], gates[:, c].rearrange("p s e -> p (s e)"), ident)
                mm.then_inc(gatesT_mm, 1)

            def moe_bias(g):
                pe.wait_ge(gatesT_ready, 1)
                if g >= 2:
                    pe.wait_ge(moe_seeded, g - 1)
                b2 = ffn[0:SETS * E, FFN_AT["b2"].start + g * D:FFN_AT["b2"].start + (g + 1) * D]
                nc.tensor.matmul(bank[6 + g % 2][:], b2, gatesT[:], start=True, stop=True).then_inc(b2_mm, 1)

            def out_bias():
                pe.wait_ge(moe_seeded, G)
                for c in range(NC):
                    mm = nc.tensor.matmul(bank[7][:, c * P:(c + 1) * P], gatesT[:, c * P:(c + 1) * P],
                                          ffn[0:SETS * E, FFN_AT["gln_b"]], start=True, stop=True)
                mm.then_inc(seed_out_mm, 1)

            def group(g):
                for s in range(STEPS):
                    if isinstance(g, int):
                        if s == 0:
                            pe.wait_ge(z_hi_ready, 1)
                            pe.wait_ge(z_lo_ready, 1)
                        up(g, s)
                        if s >= LAG:
                            down(g, s - LAG)
                        if s == LAG:
                            gates_turn()
                        if SEED_STEP <= s < SEED_STEP + 4 * G and (s - SEED_STEP) % 4 == 0:
                            moe_bias((s - SEED_STEP) // 4)
                        if s == SEED_STEP + 4 * G:
                            out_bias()
                    else:
                        up(g, s)
                        down(g, s - LAG)
                        if s == BACK_STEP:
                            back(g)

            group(0)
            with pe.Fori(1, G) as g:
                group(g)
            for s in range(-LAG, 0):
                down(G, s)
            back(G)

        @block.scalar
        def _(act):
            chain = [0]

            def link(ins):
                chain[0] += 1
                ins.then_inc(act_chain, 1)
                act.wait_ge(act_chain, chain[0])

            def root(src, tmp, dst, ready):
                link(nc.scalar.activation(tmp, src, ACT.Ln))
                nc.scalar.activation(dst, tmp, ACT.Exp, scale=-0.5).then_inc(ready, 1)

            def split_hi(e):
                nc.scalar.activation(w_hi[:, e % WSPLIT, :], w_stage[:, e, HC:], ACT.Copy).then_inc(w_hi_ready, 1)

            act.preload_act_table_set("natural_log_exp_and_others")
            act.wait_ge(noise_ready, 1)
            root(noise_abs[:], noise_log[:], noise_log[:], noise_root)
            act.wait_ge(cap_ready, 1)
            nc.scalar.activation(gate_u[:], gate_cap[:], ACT.Exp).then_inc(u_ready, 1)
            act.wait_ge(denom_ready, 1)
            link(nc.scalar.activation(gate_cap[:], gate_d[:], ACT.Ln))
            nc.scalar.activation(gate_r[:], gate_cap[:], ACT.Exp, scale=-1.0).then_inc(denom_inverse, 1)
            for e in range(AHEAD):
                act.wait_ge(w_landed[e], 16)
                split_hi(e)
            act.wait_ge(var_ready, 1)
            root(small[:, 0, :], small[:, 1, :], small[:, 2, :], root_ready)
            act.wait_ge(xhatT_mm, 1)
            nc.scalar.activation(xhatT[:], bank[3][:], ACT.Copy).then_inc(xhatT_ready, 1)
            act.wait_ge(k_ready, 1)
            for h in range(DVE_HEADS, HEADS):
                nc.scalar.activation(k_heads[:, :, h, :], qkT[:, 1, :].rearrange("p (b l) -> p b l", b=IMG), ACT.Copy,
                                     scale=mid[:, MID_AT["headmask"].start + h:MID_AT["headmask"].start + h + 1]).then_inc(k_heads_act, 1)
            for c in range(NC):
                act.wait_ge(shifted_ready, c + 1)
                nc.scalar.activation(probs[:, c, :], shifted[:, c, :], ACT.Exp, scale=float(HD) ** -0.5).then_inc(probs_ready, 1)
                for t in {2: (0,), 3: (1, 2, 3)}.get(c, ()):
                    act.wait_ge(probsT_mm, t + 1)
                    nc.scalar.activation(probsT[:, t, :], bank[PT_BANK[t]][:], ACT.Copy).then_inc(probsT_ready, 1)
            act.wait_ge(attn_mm, 1)
            nc.scalar.activation(attnT[:], bank[2][:], ACT.Identity, bias=md("bv")).then_inc(attn_ready, 1)
            act.wait_ge(var_ready, 3)
            root(small[:, 0:2, :], small[:, 2:4, :], small[:, 4:6, :], root_ready)
            act.wait_ge(shift_ready, 1)
            for c in range(NC):
                nc.scalar.activation(inp[:, c, :], h1[:, c, :], ACT.Identity, scale=small[:, 6, c:c + 1], bias=small[:, 2, c:c + 1]).then_inc(inp_ready, 1)
            act.wait_ge(inpT_mm, 1)
            nc.scalar.activation(inpT[:], bank[4][:], ACT.Copy).then_inc(inpT_ready, 1)
            act.wait_ge(zT_ready, 1)
            nc.scalar.activation(z_hi[:], zT[:], ACT.Copy).then_inc(z_hi_ready, 1)
            act.wait_ge(gap_ready, 1)
            nc.scalar.activation(top[:, 5, :], top[:, 4, :], ACT.Exp).then_inc(gap_exp, 1)
            def y_root(g):
                act.wait_ge(y_var_ready, g)
                if isinstance(g, int):
                    act.wait_ge(y_var_ready, g)
                nc.scalar.activation(y_small[:, 1, :], y_small[:, 0, :], ACT.Ln).then_inc(y_root_ready, 1)
                act.wait_ge(y_root_ready, 2 * g - 1)
                nc.scalar.activation(y_small[:, 2, :], y_small[:, 1, :], ACT.Exp, scale=-0.5).then_inc(y_root_ready, 1)

            def group(g):
                for s in range(STEPS):
                    e, c = divmod(s, HC)
                    if isinstance(g, int) and s == LAG + 1:
                        act.wait_ge(gatesT_mm, 1)
                        nc.scalar.activation(gatesT[:], bank[7][0:SETS * E, :], ACT.Copy).then_inc(gatesT_ready, 1)
                    if c == HC - 1:
                        n = e + AHEAD
                        act.wait_ge(w_landed[n % E], g * 16 + 16 * (1 + n // E))
                        reuse(act, down_done, g * STEPS + HC * (n - WSPLIT + 1))
                        split_hi(n % E)
                    act.wait_ge(up_done, g * STEPS + (s + 1))
                    reuse(act, split_done, g * STEPS + (s + 1 - RING))
                    nc.scalar.activation(relu[:, s % RING, :], bank[c][:], ACT.Relu, bias=w_stage[:, e, c:c + 1]).then_inc(relu_done, 1)
                    if c in ACT_HIGH:
                        reuse(act, down_done, g * STEPS + (s + 1 - 2 * HC))
                        act.wait_ge(relu_done, g * STEPS + (s + 1))
                        nc.scalar.activation(h_hi[:, e % 2, c, :], relu[:, s % RING, :], ACT.Copy).then_inc(act_hi_done, 1)
                    if s == Y_ROOT_STEP and not isinstance(g, int):
                        y_root(g)

            group(0)
            with act.Fori(1, G) as g:
                group(g)
            y_root(G)

        @block.gpsimd
        def _(pool):
            def split_lo(e):
                nc.gpsimd.tensor_tensor(w_lo[:, e % WSPLIT, :], w_stage[:, e, HC:], w_hi[:, e % WSPLIT, :], ALU.subtract).then_inc(w_lo_ready, 1)

            for e in range(AHEAD):
                pool.wait_ge(w_hi_ready, e + 1)
                split_lo(e)
            pool.wait_ge(mid_landed, 16)
            pool.wait_ge(h0_ready, 1)
            nc.gpsimd.tensor_tensor(h0_bproj[:], h0[:], md("bproj").unsqueeze(1).to_broadcast([P, NC, D]), ALU.add).then_inc(h0b_ready, 1)
            pool.wait_ge(rot_ready, 2)
            nc.gpsimd.tensor_tensor(qkT[:, 0, :], rot_a[:, 0, :], rot_b[:, 0, :], ALU.add).then_inc(q_ready, 1)
            for c in range(NC - 1):
                pool.wait_ge(inv_ready, c + 1)
                nc.gpsimd.tensor_tensor(probs_n[:, c, :].rearrange("p (h k) -> p h k", h=HEADS),
                                        probs[:, c, :].rearrange("p (h k) -> p h k", h=HEADS),
                                        wide(row_inv[:, c, :].unsqueeze(2), [P, HEADS, L]), ALU.mult).then_inc(probs_normed, 1)

            pool.wait_ge(z_hi_ready, 1)
            nc.gpsimd.tensor_tensor(z_lo[:], zT[:], z_hi[:], ALU.subtract).then_inc(z_lo_ready, 1)
            pool.wait_ge(inp_ready, NC)
            nc.gpsimd.tensor_tensor(out_acc[:], h1[:], inp[:], ALU.add).then_inc(out_seeded, 1)

            def sum_output(g, e):
                if isinstance(g, int):
                    g, e = g + e // E, e % E
                if isinstance(g, int) and g == 0 and e in (0, E - 1):
                    pool.wait_ge(moe_seeded, G if e else 1)
                pool.wait_ge(o_gated_ready, g * E + (e + 1))
                if not (isinstance(g, int) and g == 0 and e == 0):
                    pool.wait_ge(o_summed, g * E + e)
                if isinstance(g, int):
                    acc = moeT[:, g, :]
                else:
                    acc = moeT[:, bass.ds(g + e // E, 1), :].rearrange("p a n -> p (a n)")
                pool.sem_inc(held, 1)
                nc.gpsimd.tensor_tensor(moe_sumT[:] if e % E == E - 1 else acc, acc, o_gated[:, e % 2, :], ALU.add).then_inc(o_summed, 1)

            def group(g):
                for e in range(E):
                    if not isinstance(g, int) or e >= OUT_LAG:
                        sum_output(g, e - OUT_LAG)
                    pool.wait_ge(w_hi_ready, g * E + (e + AHEAD + 1))
                    split_lo((e + AHEAD) % E)

            group(0)
            with pool.Fori(1, G) as g:
                group(g)
            for e in range(-OUT_LAG, 0):
                sum_output(G, e)

        @block.vector
        def _(dve):
            chain = [0]

            def link(ins):
                chain[0] += 1
                ins.then_inc(dve_chain, 1)
                dve.wait_ge(dve_chain, chain[0])

            def newton(ve, y, t, out_):
                link(nc.vector.scalar_tensor_tensor(t, y, -0.5, y, ALU.mult, ALU.mult))
                link(nc.vector.tensor_tensor(t, t, ve, ALU.mult))
                link(nc.vector.scalar_tensor_tensor(out_, t, 1.5, y, ALU.add, ALU.mult))

            def token_stats(src):
                for c in range(NC):
                    ins = nc.vector.bn_stats(stats[:, c, :], src[:, c, :])
                link(ins)
                for c in range(NC):
                    ins = nc.vector.bn_aggr(mv[:, c, :], stats[:, c, :])
                link(ins)
                nc.vector.tensor_scalar(small[:, 0, :], mv[:, :, 1], EPS, None, ALU.add).then_inc(var_ready, 1)

            dve.wait_ge(tok_landed, 16)
            link(nc.vector.scalar_tensor_tensor(noise_abs[:], tok[:, 0:NOISE], -1.0, tok[:, 0:NOISE], ALU.mult, ALU.max))
            nc.vector.tensor_scalar(noise_abs[:], noise_abs[:], TINY, None, ALU.max).then_inc(noise_ready, 1)
            dve.wait_ge(noise_root, 1)
            link(nc.vector.tensor_tensor(noise_f[:], tok[:, 0:NOISE], noise_log[:], ALU.mult))
            f_in = noise_f[:, 0:KF * 2]
            f_out = noise_f[:, KF * 2:KF * 2 + 2]
            f_row = noise_f[:, KF * 2 + 2:NOISE]
            nc.vector.tensor_tensor(b_noisy[:], tk("sb"), f_out, ALU.mult).then_inc(dve_chain, 1)
            chain[0] += 1
            link(nc.vector.tensor_tensor(w_noise[:].rearrange("p (k n) -> p k n", k=KF), tk("sw").rearrange("p (k n) -> p k n", k=KF),
                                         f_row.unsqueeze(1).to_broadcast([P, KF, 2 * D]), ALU.mult))
            link(nc.vector.tensor_tensor(b_noisy[:], b_noisy[:], tk("b"), ALU.add))
            for i in range(KF * 2):
                cols = slice(i * D, (i + 1) * D)
                ins = nc.vector.scalar_tensor_tensor(w_noisy[:, cols], w_noise[:, cols], f_in[:, i:i + 1], tk("w")[:, cols], ALU.mult, ALU.add)
            ins.then_inc(weights_noisy, 1)
            dve.wait_ge(mid_landed, 16)
            link(nc.vector.tensor_tensor(pe_b3[:], md("pe"), md("b3"), ALU.add))
            dve.wait_ge(gate_mm, 1)
            nc.vector.tensor_scalar(gate_cap[:], bank[0][:], b_noisy[:, 0:1], 20.0, ALU.add, ALU.min).then_inc(cap_ready, 1)
            link(nc.vector.tensor_scalar(gate_in[:], bank[0][:], b_noisy[:, 0:1], None, ALU.add))
            dve.wait_ge(u_ready, 1)
            link(nc.vector.scalar_tensor_tensor(gate_n[:], gate_u[:], 2.0, gate_u[:], ALU.add, ALU.mult))
            nc.vector.tensor_scalar(gate_d[:], gate_n[:], 2.0, None, ALU.add).then_inc(denom_ready, 1)
            dve.wait_ge(inner_mm, 1)
            link(nc.vector.scalar_tensor_tensor(gate_in[:], bank[1][:], b_noisy[:, 1:2], gate_in[:], ALU.add, ALU.mult))
            link(nc.vector.tensor_tensor(gate_n[:], gate_n[:], gate_in[:], ALU.mult))
            dve.wait_ge(denom_inverse, 1)
            nc.vector.tensor_tensor(gated[:], gate_n[:], gate_r[:], ALU.mult).then_inc(gated_ready, 1)
            dve.wait_ge(h0_mm, 1)
            nc.vector.tensor_tensor(h0[:], bank[2][:].rearrange("p (c d) -> p c d", c=NC), pe_b3[:].unsqueeze(1).to_broadcast([P, NC, D]), ALU.add).then_inc(h0_ready, 1)
            dve.wait_ge(h0_ready, 1)
            token_stats(h0)
            dve.wait_ge(root_ready, 1)
            newton(small[:, 0, :], small[:, 2, :], small[:, 3, :], small[:, 6, :])
            for c in range(NC):
                nc.vector.tensor_scalar(xhat[:, c, :], h0[:, c, :], mv[:, c, 0:1], small[:, 6, c:c + 1], ALU.subtract, ALU.mult).then_inc(xhat_ready, 1)
            for n, (i, name, table) in enumerate([(0, "q", "cos"), (0, "qs", "sin"), (1, "k", "cos"), (1, "ks", "sin")]):
                src = {"q": 0, "qs": 1, "k": 2, "ks": 3}[name]
                dst = rot_a if table == "cos" else rot_b
                dve.wait_ge(qk_mm, src + 1)
                turned = (nc.vector.scalar_tensor_tensor(dst[:, i, :].rearrange("p (b l) -> p b l", b=IMG), bank[4 + src][:].rearrange("p (b l) -> p b l", b=IMG),
                                                    mid[:, MID_AT["bqkv"].start + src:MID_AT["bqkv"].start + src + 1],
                                                    md(table).unsqueeze(1).to_broadcast([P, IMG, L]), ALU.add, ALU.mult))
                if i == 0:
                    turned.then_inc(rot_ready, 1)
                elif table == "cos":
                    turned.then_inc(dve_chain, 1)
                    chain[0] += 1
                else:
                    link(turned)
                    nc.vector.tensor_tensor(qkT[:, i, :], rot_a[:, i, :], rot_b[:, i, :], ALU.add).then_inc(k_ready, 1)
                    dve.wait_ge(k_ready, 1)
                    for h in range(DVE_HEADS):
                        nc.vector.tensor_scalar(k_heads[:, :, h, :], qkT[:, 1, :].rearrange("p (b l) -> p b l", b=IMG),
                                                mid[:, MID_AT["headmask"].start + h:MID_AT["headmask"].start + h + 1], None, ALU.mult).then_inc(k_heads_dve, 1)
            for i in range(2):
                dve.wait_ge(v_mm, i + 1)
                nc.vector.tensor_tensor(v_heads[:, 4 * i:4 * i + 4, :], bank[i][:].rearrange("p (b d) -> p b d", b=4),
                                        md("parmask").unsqueeze(1).to_broadcast([P, 4, D]), ALU.mult).then_inc(v_ready, 1)
            def soft_sum(c):
                dve.wait_ge(probs_ready, c + 1)
                link(nc.vector.tensor_reduce(row_sum[:, c, :], probs[:, c, :].rearrange("p (h k) -> p h k", h=HEADS), AX.X, ALU.add))
                nc.vector.reciprocal(row_inv[:, c, :], row_sum[:, c, :]).then_inc(inv_ready, 1)

            for c in range(NC):
                dve.wait_ge(scores_mm, c + 1)
                s3 = bank[2 + c][:].rearrange("p (h k) -> p h k", h=HEADS)
                link(nc.vector.tensor_reduce(row_max[:, c, :], s3, AX.X, ALU.max))
                nc.vector.tensor_tensor(shifted[:, c, :].rearrange("p (h k) -> p h k", h=HEADS), s3,
                                        wide(row_max[:, c, :].unsqueeze(2), [P, HEADS, L]), ALU.subtract).then_inc(shifted_ready, 1)
                if c >= 1:
                    soft_sum(c - 1)
            soft_sum(NC - 1)
            dve.wait_ge(inv_ready, NC)
            nc.vector.tensor_tensor(probs_n[:, NC - 1, :].rearrange("p (h k) -> p h k", h=HEADS),
                                    probs[:, NC - 1, :].rearrange("p (h k) -> p h k", h=HEADS),
                                    wide(row_inv[:, NC - 1, :].unsqueeze(2), [P, HEADS, L]), ALU.mult).then_inc(last_probs_normed, 1)
            dve.wait_ge(proj_mm, 1)
            dve.wait_ge(h0b_ready, 1)
            link(nc.vector.tensor_tensor(h1[:], bank[3][:].rearrange("p (c d) -> p c d", c=NC), h0_bproj[:], ALU.add))
            token_stats(h1)
            dve.wait_ge(var_ready, 2)
            link(nc.vector.reciprocal(small[:, 7, :], small[:, 0, :]))
            link(nc.vector.tensor_tensor(small[:, 7, :], small[:, 7, :], mv[:, :, 1], ALU.mult))
            nc.vector.tensor_scalar(small[:, 1, :], small[:, 7, :], EPS, None, ALU.add).then_inc(var_ready, 1)
            dve.wait_ge(root_ready, 2)
            newton(small[:, 0:2, :], small[:, 4:6, :], small[:, 2:4, :], small[:, 6:8, :])
            nc.vector.scalar_tensor_tensor(small[:, 2, :], mv[:, :, 0], -1.0, small[:, 6, :], ALU.mult, ALU.mult).then_inc(shift_ready, 1)
            link(nc.vector.tensor_tensor(small[:, 3, :], small[:, 6, :], small[:, 7, :], ALU.mult))
            for c in range(NC):
                nc.vector.tensor_scalar(zhat[:, c, :], h1[:, c, :], mv[:, c, 0:1], small[:, 3, c:c + 1], ALU.subtract, ALU.mult).then_inc(zhat_ready, 1)
            dve.wait_ge(ffn_landed, 16)
            dve.wait_ge(zT_mm, 1)
            nc.vector.tensor_scalar(zT[:], bank[5][:], ff("ln_g"), ff("ln_b"), ALU.mult, ALU.add).then_inc(zT_ready, 1)
            flat = lambda t: t[:].rearrange("p c s e -> p (c s) e")
            spread = lambda ap: ap.unsqueeze(2).to_broadcast([P, NC * SETS, E])
            order = ff("order").unsqueeze(1).to_broadcast([P, NC * SETS, E])
            chain[0] += 2
            nc.vector.memset(logits[:, :, G, G:E], -1e30).then_inc(dve_chain, 1)
            dve.wait_ge(logits_mm, 1)
            nc.vector.tensor_copy(logits[:, :, G, 0:G], bank[6][:, 0:NC * G].rearrange("p (c g) -> p c g", c=NC)).then_inc(dve_chain, 1)
            link(nc.vector.tensor_copy(logits[:].rearrange("p c s e -> p c (s e)")[:, :, 0:G * E],
                                       bank[6][:, 128:128 + NC * G * E].rearrange("p (c x) -> p c x", c=NC)))
            link(nc.vector.tensor_reduce(top[:, 0, :], flat(logits), AX.X, ALU.max))
            link(nc.vector.tensor_tensor(flat(equal), flat(logits), spread(top[:, 0, :]), ALU.is_equal))
            link(nc.vector.tensor_tensor(flat(key), flat(equal), order, ALU.mult))
            link(nc.vector.tensor_reduce(top[:, 1, :], flat(key), AX.X, ALU.max))
            link(nc.vector.tensor_tensor(flat(first), flat(key), spread(top[:, 1, :]), ALU.is_equal))
            link(nc.vector.scalar_tensor_tensor(flat(rest), flat(first), -1e38, flat(logits), ALU.mult, ALU.add))
            link(nc.vector.tensor_reduce(top[:, 2, :], flat(rest), AX.X, ALU.max))
            nc.vector.tensor_tensor(top[:, 4, :], top[:, 2, :], top[:, 0, :], ALU.subtract).then_inc(gap_ready, 1)
            link(nc.vector.tensor_tensor(flat(equal), flat(rest), spread(top[:, 2, :]), ALU.is_equal))
            link(nc.vector.tensor_tensor(flat(key), flat(equal), order, ALU.mult))
            link(nc.vector.tensor_reduce(top[:, 3, :], flat(key), AX.X, ALU.max))
            link(nc.vector.tensor_tensor(flat(second), flat(key), spread(top[:, 3, :]), ALU.is_equal))
            dve.wait_ge(gap_exp, 1)
            link(nc.vector.tensor_scalar(top[:, 6, :], top[:, 5, :], 1.0, None, ALU.add))
            link(nc.vector.reciprocal(top[:, 7, :], top[:, 6, :]))
            link(nc.vector.tensor_tensor(top[:, 6, :], top[:, 5, :], top[:, 7, :], ALU.mult))
            link(nc.vector.tensor_tensor(flat(first), flat(first), spread(top[:, 7, :]), ALU.mult))
            link(nc.vector.tensor_tensor(flat(second), flat(second), spread(top[:, 6, :]), ALU.mult))
            nc.vector.tensor_tensor(flat(gates), flat(first), flat(second), ALU.add).then_inc(gates_ready, 1)

            def seed(g):
                dve.wait_ge(b2_mm, g + 1)
                nc.vector.tensor_tensor(moeT[:, g, :], bank[6 + g % 2][:], zT[:], ALU.add).then_inc(moe_seeded, 1)

            def seed_out():
                dve.wait_ge(out_seeded, 1)
                dve.wait_ge(seed_out_mm, 1)
                link(nc.vector.tensor_tensor(out_acc[:], bank[7][:].rearrange("p (c d) -> p c d", c=NC), out_acc[:], ALU.add))

            def high(g, s):
                e, c = divmod(s, HC)
                dve.wait_ge(relu_done, g * STEPS + (s + 1))
                reuse(dve, down_done, g * STEPS + (s + 1 - 2 * HC))
                nc.vector.tensor_copy(h_hi[:, e % 2, c, :], relu[:, s % RING, :]).then_inc(hi_done, 1)

            def low(g, s):
                e, c = divmod(s, HC)
                own = HC - len(ACT_HIGH)
                if c in ACT_HIGH:
                    dve.wait_ge(act_hi_done, g * (E * len(ACT_HIGH)) + (e * len(ACT_HIGH) + sorted(ACT_HIGH).index(c) + 1))
                else:
                    dve.wait_ge(hi_done, g * (E * own) + (e * own + [x for x in range(HC) if x not in ACT_HIGH].index(c) + 1))
                nc.vector.tensor_tensor(h_lo[:, e % 2, c, :], relu[:, s % RING, :], h_hi[:, e % 2, c, :], ALU.subtract).then_inc(split_done, 1)

            def gate_output(g, e):
                dve.wait_ge(down_done, g * STEPS + HC * (e + 1))
                dve.wait_ge(iw_landed[e % E], g * 16 + (16 if e >= 0 else 0))
                reuse(dve, o_summed, g * E + (e - 1))
                nc.vector.tensor_tensor(o_gated[:, e % 2, :], bank[4 + e % 2][:], iw_rows[:, e % E, :], ALU.mult).then_inc(o_gated_ready, 1)

            y3 = bank[6][:].rearrange("p (c d) -> p c d", c=NC)
            YLINKS = 9
            Y_PARTS = 6
            Y_AT = {12: 0, 16: 1, 20: 2, 24: 3, 28: 4, 30: 5}
            SEED_AT = {8: 0, 12: 1, 16: 2, 20: 3}

            def y_link(ins, g, n):
                ins.then_inc(yT_read, 1)
                dve.wait_ge(yT_read, g * YLINKS + (n + 1 - YLINKS))

            def y_out(g, part):
                if part == 0:
                    dve.wait_ge(yT_mm, g)
                    for c in range(NC):
                        ins = nc.vector.bn_stats(y_stats[:, c, :], y3[:, c, :])
                    y_link(ins, g, 0)
                if part == 1:
                    dve.sem_inc(held, 1)
                    for c in range(NC):
                        ins = nc.vector.bn_aggr(y_mv[:, c, :], y_stats[:, c, :])
                    y_link(ins, g, 1)
                    nc.vector.tensor_scalar(y_small[:, 0, :], y_mv[:, :, 1], EPS, None, ALU.add).then_inc(y_var_ready, 1)
                if part == 2:
                    dve.wait_ge(y_root_ready, 2 * g)
                    y = y_small[:, 2, :]
                    y_link(nc.vector.scalar_tensor_tensor(y_small[:, 3, :], y, -0.5, y, ALU.mult, ALU.mult), g, 2)
                    y_link(nc.vector.tensor_tensor(y_small[:, 3, :], y_small[:, 3, :], y_small[:, 0, :], ALU.mult), g, 3)
                    y_link(nc.vector.scalar_tensor_tensor(y_small[:, 4, :], y_small[:, 3, :], 1.5, y, ALU.add, ALU.mult), g, 4)
                    if isinstance(g, int):
                        gw = gates[:, :, G, g - 1]
                    else:
                        gw = gates[:, :, G, bass.ds(g - 1, 1)].rearrange("p c a -> p (c a)")
                    y_link(nc.vector.tensor_tensor(y_small[:, 5, :], y_small[:, 4, :], gw, ALU.mult), g, 5)
                if part == 3:
                    for c in range(NC):
                        ins = nc.vector.tensor_scalar(y_hat[:, c, :], y3[:, c, :], y_mv[:, c, 0:1], y_small[:, 5, c:c + 1], ALU.subtract, ALU.mult)
                    y_link(ins, g, 6)
                if part == 4:
                    if isinstance(g, int):
                        gain = ffn[:, FFN_AT["gln_g"].start + (g - 1) * D:FFN_AT["gln_g"].start + g * D].unsqueeze(1)
                    else:
                        gain = ff("gln_g").rearrange("p (g d) -> p g d", g=G)[:, bass.ds(g - 1, 1), :]
                    y_link(nc.vector.tensor_tensor(y_scaled[:], y_hat[:], gain.to_broadcast([P, NC, D]), ALU.mult), g, 7)
                if part == 5:
                    y_link(nc.vector.tensor_tensor(out_acc[:], out_acc[:], y_scaled[:], ALU.add), g, 8)

            def group(g):
                for s in range(STEPS):
                    if s % HC not in ACT_HIGH:
                        high(g, s)
                    low(g, s)
                    if isinstance(g, int):
                        if s in SEED_AT:
                            seed(SEED_AT[s])
                        if s == 24:
                            seed_out()
                    if s % HC == 2 and (s >= 2 * HC or not isinstance(g, int)):
                        gate_output(g, s // HC - 2)
                    if not isinstance(g, int) and s in Y_AT:
                        y_out(g, Y_AT[s])

            group(0)
            with dve.Fori(1, G) as g:
                group(g)
            gate_output(G, -2)
            gate_output(G, -1)
            for part in range(Y_PARTS):
                y_out(G, part)
            nc.vector.engine_nop().then_inc(out_ready, 1)


def shape_tables():
    pos = np.arange(L, dtype=np.float32)[:, None]
    div = np.exp(np.arange(0, D, 2, dtype=np.float32) * np.float32(-np.log(10000.0) / D)).astype(np.float32)
    ang = (pos * div).astype(np.float32)
    pe = np.stack([np.sin(ang), np.cos(ang)], axis=-1).reshape(L, D).astype(np.float32)
    freqs = (1.0 / np.float32(10000.0) ** (np.arange(0, HD, 2, dtype=np.float32) / HD)).astype(np.float32)
    turn = np.outer(np.arange(L, dtype=np.float32), freqs).astype(np.float32)
    dim = np.arange(D) % HD
    cos = np.cos(turn)[:, dim // 2].T.astype(np.float32)
    sin = (np.sin(turn)[:, dim // 2].T * np.where(dim % 2 == 0, -1.0, 1.0)[:, None]).astype(np.float32)
    p = np.arange(P)
    headmask = (p[:, None] // HD == np.arange(HEADS)[None, :]).astype(np.float32)
    parmask = (p[:, None] // L == (np.arange(D)[None, :] // HD) % 2).astype(np.float32)
    order = np.tile(np.arange(E, 0, -1, dtype=np.float32), (P, 1))
    return {"pe": np.concatenate([pe] * (P // L)), "cos": cos, "sin": sin, "headmask": headmask,
            "parmask": parmask, "order": order, "ident": np.eye(P, dtype=np.float32)}


def kernel(**inputs):
    import concourse.bacc as bacc
    from concourse.bass_utils import run_bass_kernel_spmd

    a = {k: np.asarray(v) for k, v in inputs.items()}
    t = shape_tables()

    def rows(v):
        return np.broadcast_to(v.reshape(1, -1), (P, v.size))

    def pack(parts, values):
        return np.ascontiguousarray(np.concatenate([values[n].reshape(P, w) for n, w in parts], axis=1))

    def feat(wa, wb):
        return np.stack([wa, wb]).reshape(2, D, KF, P).transpose(3, 2, 0, 1)

    x = a["x"].reshape(IMG, SIDE, PATCH, SIDE, PATCH).transpose(2, 4, 0, 1, 3).reshape(KF, P, N).transpose(1, 0, 2)
    tok = {
        "noise_in": np.stack([a["L0_tok_eps_in1"], a["L0_tok_eps_in2"]]).reshape(2, KF, P).transpose(2, 1, 0),
        "noise_out": np.stack([a["L0_tok_eps_out1"], a["L0_tok_eps_out2"]], axis=1),
        "noise_row": rows(np.stack([a["L0_tok_eps_out1"], a["L0_tok_eps_out2"]])),
        "b": np.stack([a["L0_tok_W1_b"], a["L0_tok_W2_b"]], axis=1),
        "sb": np.stack([a["L0_tok_W1_sb"], a["L0_tok_W2_sb"]], axis=1),
        "w": feat(a["L0_tok_W1_w"], a["L0_tok_W2_w"]),
        "sw": feat(a["L0_tok_W1_sw"], a["L0_tok_W2_sw"]),
    }
    swap = np.arange(D) ^ 1
    wq, wk, wv = a["L0_attn_Wqkv"].reshape(3, D, D)
    bq, bk, bv = a["L0_attn_bqkv"].reshape(3, D)
    mid = {
        "w3T": a["L0_tok_W3_w"].T, "b3": rows(a["L0_tok_W3_b"]), "pe": t["pe"], "ident": t["ident"],
        "wqkvT": np.concatenate([wq.T, wq[swap].T, wk.T, wk[swap].T, wv.T], axis=1),
        "bqkv": np.stack([bq, bq[swap], bk, bk[swap]], axis=1), "bv": bv,
        "cos": t["cos"], "sin": t["sin"], "headmask": t["headmask"], "parmask": t["parmask"],
        "wprojT": a["L0_attn_Wproj"].T, "bproj": rows(a["L0_attn_bproj"]),
    }
    b2 = np.zeros((P, G, D), np.float32)
    for g in range(G):
        b2[g * E:(g + 1) * E, g] = a["L0_ffn_b2"][g]
    gln_b = np.zeros((P, D), np.float32)
    gln_b[G * E:G * E + G] = a["L0_ffn_gln_b"]
    ffn = {
        "wg": a["L0_ffn_wg_group"], "wgi": a["L0_ffn_wg_inner"].transpose(1, 0, 2), "ln_g": a["L0_ffn_ln_g"],
        "ln_b": a["L0_ffn_ln_b"], "order": t["order"], "gln_g": rows(a["L0_ffn_gln_g"]), "gln_b": gln_b, "b2": b2,
    }
    experts = np.concatenate([
        a["L0_ffn_b1"].reshape(G * E, HC, P).transpose(0, 2, 1),
        a["L0_ffn_W1"].reshape(G * E, D, H),
        a["L0_ffn_W2"].reshape(G * E, HC, P, D).transpose(0, 2, 1, 3).reshape(G * E, P, H)], axis=2)
    arrays = {"tok_in": pack(TOK_PARTS, tok), "x_in": np.ascontiguousarray(x), "mid_in": pack(MID_PARTS, mid), "ffn_in": pack(FFN_PARTS, ffn),
              "experts_in": np.ascontiguousarray(experts)}

    nc = bacc.Bacc("TRN2", target_bir_lowering=False, num_devices=1)
    args = [nc.dram_tensor(n, v.shape, F32, kind="ExternalInput").ap() for n, v in arrays.items()]
    out = nc.dram_tensor("out", (N, D), F32, kind="ExternalOutput").ap()
    vit_tower(nc, *args, out)
    r = run_bass_kernel_spmd(nc, [arrays], core_ids=[0])
    return r.results[0]["out"].reshape(IMG, L, D)
```

```python
from contextlib import ExitStack

import numpy as np

import concourse.bass as bass
from concourse import mybir

F32 = mybir.dt.float32
F16 = mybir.dt.float16
ALU = mybir.AluOpType
ACT = mybir.ActivationFunctionType
AX = mybir.AxisListType

P = 128
IMG, PIX, PATCH = 8, 128, 16
SIDE = PIX // PATCH
L = SIDE * SIDE
N = IMG * L
NC = N // P
FEAT = PATCH * PATCH
KF = FEAT // P
D = 128
HEADS = 8
HD = D // HEADS
G, E, H = 4, 8, 512
HC = H // P
SETS = G + 1
EPS = 1e-5
TINY = 2.0 ** -60
B2_AT, W_AT = HC, 8
WCOLS = W_AT + 2 * H
WSPLIT, AHEAD = 4, 2
STEPS, LAG, OUT_LAG = E * HC, 6, 2
RING = 8
ACT_HIGH = (0, 2)
BACK_STEP, Y_ROOT_STEP = 11, 18
MASKS, POOL_MASKS = HEADS // 2, 1
UNITS = 2 * HEADS // MASKS
EARLY, LOGITS_STEP, GAP_STEP, GATES_STEP, SEED_STEP = 5, 1, 3, 8, 12
WARM = {"weights": 11, "gated": 14, "xhat": 15, "zhat": 14, "z": 3}
PT_BANK = [6, 7, 0, 1]
ATTN_BANK, SUM_BANK = [2, 4], [3, 5]
PROJ_BANK = [6, 0, 7, 1]
H0_BANK = [4, 5, 0, 1]


def columns(parts):
    at, where = 0, {}
    for name, width in parts:
        where[name] = slice(at, at + width)
        at += width
    return where, at


TOK_PARTS = [("noise_in", KF * 2), ("noise_out", 2), ("noise_row", 2 * D), ("b", 2), ("sb", 2), ("w", KF * 2 * D),
             ("sw", KF * 2 * D)]
MID_PARTS = [("w3T", D), ("b3", D), ("pe", D), ("ident", D), ("wqkvT", 6 * D), ("bqkv", 4), ("bv_cols", P),
             ("cos", L), ("sin", L), ("headmask", HEADS // 2), ("parmask", D), ("wprojT", D), ("bproj", D)]
FFN_PARTS = [("wg", G), ("wgi", G * E), ("ln_g", 1), ("ln_b", 1), ("order", E), ("gln_g", G * D), ("gln_b", D)]
TOK_AT, TOK_W = columns(TOK_PARTS)
MID_AT, MID_W = columns(MID_PARTS)
FFN_AT, FFN_W = columns(FFN_PARTS)


def vit_tower(nc, tok_in, x_in, mid_in, ffn_in, experts, out):
    ctx = ExitStack()
    with ctx:
        def sb(name, shape, dt=F32):
            return ctx.enter_context(nc.sbuf_tensor(name, shape, dt))

        def sem(name):
            return ctx.enter_context(nc.semaphore(name))

        bank = [ctx.enter_context(nc.psum_tensor(f"bank{i}", [P, 512], F32)) for i in range(8)]
        gates_dram = nc.dram_tensor("gates_t", [G * E, N], F32)

        tok = sb("tok", [P, TOK_W])
        patches = sb("patches", [P, KF, N])
        mid = sb("mid", [P, MID_W])
        ffn = sb("ffn", [P, FFN_W])

        def tk(name):
            return tok[:, TOK_AT[name]]

        def md(name):
            return mid[:, MID_AT[name]]

        def ff(name):
            return ffn[:, FFN_AT[name]]

        NOISE = KF * 2 + 2 + 2 * D
        noise_abs = sb("noise_abs", [P, NOISE])
        noise_log = sb("noise_log", [P, NOISE])
        noise_f = sb("noise_f", [P, NOISE])
        w_noise = sb("w_noise", [P, KF * 2 * D])
        w_noisy = sb("w_noisy", [P, KF * 2 * D])
        b_noisy = sb("b_noisy", [P, 2])
        gate_in = sb("gate_in", [P, N])
        gate_cap = sb("gate_cap", [P, N])
        gate_u = sb("gate_u", [P, N])
        gate_n = sb("gate_n", [P, N])
        gate_in_inner = sb("gate_in_inner", [P, N])
        ln_bias = sb("ln_bias", [P, 4])
        warm = sb("warm", [P, N], F16)
        gate_r = sb("gate_r", [P, N])
        gated = sb("gated", [P, N])
        pe_b3 = sb("pe_b3", [P, D])
        h0 = sb("h0", [P, NC, D])
        h0_bproj = sb("h0_bproj", [P, NC, D])
        stats = sb("stats", [P, NC, 6])
        mv = sb("mv", [P, NC, 2])
        small = sb("small", [P, 8, NC])
        xhat = sb("xhat", [P, NC, D])
        xhatT = sb("xhatT", [P, N])
        rot_a = sb("rot_a", [P, 2, N])
        rot_b = sb("rot_b", [P, 2, N])
        qkT = sb("qkT", [P, 2, N])
        iw_rows = sb("iw_rows", [P, E, N])
        k_heads = iw_rows[:].rearrange("p e n -> p (e n)")[:, 0:IMG * MASKS * L].rearrange("p (b h k) -> p b h k", b=IMG, h=MASKS)
        v_heads = sb("v_heads", [P, IMG, D])
        row_max = sb("row_max", [P, NC, HEADS])
        shifted = sb("shifted", [P, NC, HEADS * L])
        probs_both = sb("probs_both", [P, 2, NC, HEADS * L])
        probs, probsT = probs_both[:, 0], probs_both[:, 1]
        h_lo_store = sb("h_lo_store", [P, NC, N])
        sum_log, sum_inv = gate_u, gate_r
        attnT = sb("attnT", [P, N])
        h1 = sb("h1", [P, NC, D])
        zhat = sb("zhat", [P, NC, D])
        zhatT = sb("zhatT", [P, N])
        zT = sb("zT", [P, N])
        wgi_hi = sb("wgi_hi", [P, G * E], F16)
        wgi_lo = sb("wgi_lo", [P, G * E], F16)
        z_hi = sb("z_hi", [P, N], F16)
        z_lo = sb("z_lo", [P, N], F16)
        logits = sb("logits", [P, NC, SETS, E])
        rest = sb("rest", [P, NC, SETS, E])
        equal = sb("equal", [P, NC, SETS, E])
        key = sb("key", [P, NC, SETS, E])
        first = sb("first", [P, NC, SETS, E])
        second = sb("second", [P, NC, SETS, E])
        gates = sb("gates", [P, NC, SETS, E])
        top = sb("top", [P, 8, NC * SETS])
        gatesT = sb("gatesT", [SETS * E, N])
        out_acc = sb("out_acc", [P, NC, D])

        w_stage = sb("w_stage", [P, E, WCOLS])
        minus_b1 = sb("minus_b1", [P, E, HC])
        w_hi = sb("w_hi", [P, WSPLIT, 2 * H], F16)
        w_lo = sb("w_lo", [P, WSPLIT, 2 * H], F16)
        relu = probs_both[:].rearrange("p t c n -> p (t c) n")
        h_hi = shifted[:].rearrange("p c n -> p (c n)").bitcast(F16).rearrange("p (t c n) -> p t c n", t=2, c=HC)
        h_lo = h_lo_store[:].rearrange("p c n -> p (c n)").bitcast(F16).rearrange("p (t c n) -> p t c n", t=2, c=HC)
        o_gated = sb("o_gated", [P, 2, N])
        moe_accT = sb("moe_accT", [P, N])
        moe_sumT = sb("moe_sumT", [P, N])
        y_stats = sb("y_stats", [P, NC, 6])
        y_mv = sb("y_mv", [P, NC, 2])
        y_small = sb("y_small", [P, 6, NC])
        y_gain = sb("y_gain", [P, NC, D])

        x_landed, noise_landed = [sem("x_landed0"), sem("x_landed1")], sem("noise_landed")
        pe_b3_ready = sem("pe_b3_ready")
        tok_landed, mid_landed, ffn_landed = sem("tok_landed"), sem("mid_landed"), sem("ffn_landed")
        w_landed = [sem(f"w_landed{i}") for i in range(E)]
        iw_landed = [sem(f"iw_landed{i}") for i in range(E)]
        gates_stored, out_stored = sem("gates_stored"), sem("out_stored")
        dve_chain, act_chain, pool_chain = sem("dve_chain"), sem("act_chain"), sem("pool_chain")
        noise_ready, noise_root = sem("noise_ready"), sem("noise_root")
        weights_noisy = sem("weights_noisy")
        gate_mm, inner_mm = sem("gate_mm"), sem("inner_mm")
        cap_ready, u_ready = sem("cap_ready"), sem("u_ready")
        gate_copied, n_ready, m_ready = sem("gate_copied"), sem("n_ready"), sem("m_ready")
        denom_inverse, mn_ready = sem("denom_inverse"), sem("mn_ready")
        constants_set = sem("constants_set")
        gated_ready, h0_mm, h0_ready = sem("gated_ready"), sem("h0_mm"), sem("h0_ready")
        h0b_ready, h1_ready = sem("h0b_ready"), sem("h1_ready")
        var_ready, root_ready = sem("var_ready"), sem("root_ready")
        xhat_ready, xhatT_mm, xhatT_ready = sem("xhat_ready"), sem("xhatT_mm"), sem("xhatT_ready")
        qk_mm, v_mm = sem("qk_mm"), sem("v_mm")
        rot_ready, q_ready, k_ready = sem("rot_ready"), sem("q_ready"), sem("k_ready")
        k_heads_pool, k_heads_act, v_ready = sem("k_heads_pool"), sem("k_heads_act"), sem("v_ready")
        scores_mm, shifted_ready, probs_ready = sem("scores_mm"), sem("shifted_ready"), sem("probs_ready")
        sums_mm, sums_inverse = sem("sums_mm"), sem("sums_inverse")
        probsT_mm, probsT_ready = sem("probsT_mm"), sem("probsT_ready")
        attn_mm, attn_ready, proj_mm = sem("attn_mm"), sem("attn_ready"), sem("proj_mm")
        out_seeded = sem("out_seeded")
        zhatT_ready = sem("zhatT_ready")
        wgi_hi_ready, wgi_lo_ready = sem("wgi_hi_ready"), sem("wgi_lo_ready")
        zhat_ready, zT_mm, zT_ready = sem("zhat_ready"), sem("zT_mm"), sem("zT_ready")
        z_hi_ready, z_lo_ready = sem("z_hi_ready"), sem("z_lo_ready")
        logits_mm, gap_ready, gap_exp = sem("logits_mm"), sem("gap_ready"), sem("gap_exp")
        gates_ready, gatesT_mm, gatesT_ready = sem("gates_ready"), sem("gatesT_mm"), sem("gatesT_ready")
        seed_out_mm = sem("seed_out_mm")
        w_hi_ready, w_lo_ready, minus_b1_ready = sem("w_hi_ready"), sem("w_lo_ready"), sem("minus_b1_ready")
        up_done, relu_done = sem("up_done"), sem("relu_done")
        act_hi_done = sem("act_hi_done")
        hi_done, split_done, down_done = sem("hi_done"), sem("split_done"), sem("down_done")
        o_gated_ready, o_summed = sem("o_gated_ready"), sem("o_summed")
        yT_mm, y_var_ready, y_root_ready, yT_read = sem("yT_mm"), sem("y_var_ready"), sem("y_root_ready"), sem("yT_read")
        out_ready, last_gated = sem("out_ready"), sem("last_gated")
        held = sem("held")

        ident = md("ident")

        def half_cols(half):
            return slice(half * N // 2, (half + 1) * N // 2)

        block = ctx.enter_context(nc.Block())

        def wide(ap, shape):
            return ap.to_broadcast(shape)

        def reuse(eng, signal, count):
            if not isinstance(count, int) or count > 0:
                eng.wait_ge(signal, count)

        def from_psum(g, s):
            return s % HC in ACT_HIGH and not (isinstance(g, int) and s < EARLY)

        def high_made(eng, g, s):
            e, c = divmod(s, HC)
            others = [x for x in range(HC) if x not in ACT_HIGH]
            if c in ACT_HIGH:
                eng.wait_ge(act_hi_done, g * (E * len(ACT_HIGH)) + (e * len(ACT_HIGH) + ACT_HIGH.index(c) + 1))
            else:
                eng.wait_ge(hi_done, g * (E * len(others)) + (e * len(others) + others.index(c) + 1))

        @block.sync
        def _(sync):
            first = TOK_AT["w"].start
            sync.dma_start(tok[:, 0:first], tok_in[:, 0:first]).then_inc(noise_landed, 16)
            sync.dma_start(tok[:, first:], tok_in[:, first:]).then_inc(tok_landed, 16)
            for half in range(2):
                sync.dma_start(patches[:, :, half_cols(half)], x_in[:, :, half_cols(half)]).then_inc(x_landed[half], 16)
            sync.dma_start(mid[:], mid_in).then_inc(mid_landed, 16)
            sync.dma_start(w_stage[:, 0, :], experts[0]).then_inc(w_landed[0], 16)
            sync.dma_start(ffn[:], ffn_in).then_inc(ffn_landed, 16)
            for e in range(1, E):
                sync.dma_start(w_stage[:, e, :], experts[e]).then_inc(w_landed[e], 16)
            sync.wait_ge(gatesT_ready, 1)
            sync.dma_start(gates_dram[:, :], gatesT[0:G * E, :]).then_inc(gates_stored, 16)
            sync.wait_ge(gates_stored, 16)
            for e in range(E):
                sync.dma_start(iw_rows[:, e, :], gates_dram[e:e + 1, :].to_broadcast([P, N])).then_inc(iw_landed[e], 16)
            with sync.Fori(1, G) as g:
                for e in range(E):
                    expert = sync.snap(g * E + e)
                    through = sync.snap(g * E + (e + 1 - E))
                    sync.wait_ge(o_gated_ready, through)
                    sync.sem_inc(held, 1)
                    sync.dma_start(w_stage[:, e, :], experts[bass.ds(expert, 1), :, :].squeeze(0)).then_inc(w_landed[e], 16)
                    sync.dma_start(iw_rows[:, e, :], gates_dram[bass.ds(expert, 1), :].to_broadcast([P, N])).then_inc(iw_landed[e], 16)
            for e in range(AHEAD):
                sync.wait_ge(w_lo_ready, (G - 1) * E + e + 1)
                sync.wait_ge(relu_done, (G - 1) * STEPS + HC * (e + 1))
                sync.dma_start(w_stage[:, e, 0:HC], experts[e, :, 0:HC]).then_inc(w_landed[e], 16)
            for half in range(2):
                sync.wait_ge(out_ready, 2 * half + 2)
                sync.dma_start(out.rearrange("(c p) d -> p c d", p=P)[:, 2 * half:2 * half + 2], out_acc[:, 2 * half:2 * half + 2]).then_inc(out_stored, 16)
            sync.wait_ge(out_stored, 32)

        @block.tensor
        def _(pe):
            def keep_warm(n, spare):
                for _ in range(n):
                    nc.tensor.matmul(bank[spare][:], warm[:, 0:P], warm[:], start=True, stop=True)

            pe.wait_ge(constants_set, 1)
            keep_warm(WARM["weights"], 7)
            wn = w_noisy[:].rearrange("p (k w h) -> p k w h", k=KF, w=2)
            for w, done in ((0, gate_mm), (1, inner_mm)):
                pe.wait_ge(weights_noisy, w + 1)
                for half in range(2):
                    pe.wait_ge(x_landed[half], 16)
                    for k in range(KF):
                        mm = nc.tensor.matmul(bank[2 * w + half][:, 0:N // 2], wn[:, k, w, :], patches[:, k, half_cols(half)],
                                              start=(k == 0), stop=(k == KF - 1))
                    mm.then_inc(done, 1)
            keep_warm(WARM["gated"], 7)
            pe.wait_ge(mid_landed, 16)
            for c in range(NC):
                pe.wait_ge(gated_ready, c // 2 + 1)
                nc.tensor.matmul(bank[H0_BANK[c]][:, c * P:(c + 1) * P], gated[:, c * P:(c + 1) * P], md("w3T"), start=True, stop=True).then_inc(h0_mm, 1)
            keep_warm(WARM["xhat"], 2)
            for c in range(NC):
                pe.wait_ge(xhat_ready, c + 1)
                nc.tensor.transpose(bank[6 + c // 2][:, c * P:(c + 1) * P], xhat[:, c, :], ident).then_inc(xhatT_mm, 1)
            pe.wait_ge(xhatT_ready, 2)
            for i in range(4):
                w = mid[:, MID_AT["wqkvT"].start + i * D:MID_AT["wqkvT"].start + (i + 1) * D]
                nc.tensor.matmul(bank[4 + i][:], w, xhatT[:], start=True, stop=True).then_inc(qk_mm, 1)
            for b in range(IMG):
                for half in range(2):
                    wv = mid[:, MID_AT["wqkvT"].start + (4 + half) * D:MID_AT["wqkvT"].start + (5 + half) * D]
                    v = bank[b // 4][half * L:(half + 1) * L, (b % 4) * D:(b % 4 + 1) * D]
                    mm = nc.tensor.matmul(v, xhatT[:, b * L:(b + 1) * L], wv, start=True, stop=True)
                if b % 4 == 3:
                    mm.then_inc(v_mm, 1)
            pe.wait_ge(q_ready, 1)
            pe.wait_ge(k_heads_pool, POOL_MASKS)
            pe.wait_ge(k_heads_act, MASKS - POOL_MASKS)
            pe.wait_ge(h0_ready, NC)
            for u in range(UNITS):
                rows = slice(u % 2 * D // 2, (u % 2 + 1) * D // 2)
                for pair in range(2):
                    for half in range(2):
                        b = 4 * (u // 2) + 2 * pair + half
                        mm = nc.tensor.matmul(bank[2 + u][half * L:(half + 1) * L, pair * MASKS * L:(pair + 1) * MASKS * L],
                                              qkT[rows, 1, b * L:(b + 1) * L], k_heads[rows, b].rearrange("p h k -> p (h k)"), start=True, stop=True)
                mm.then_inc(scores_mm, 1)
            pe.wait_ge(v_ready, 2)
            for u in range(UNITS + 1):
                if u < UNITS:
                    pe.wait_ge(probs_ready, u + 1)
                    for i in range(4):
                        mm = nc.tensor.transpose(bank[PT_BANK[u]][:, i * P:(i + 1) * P], probs[:, u, i * P:(i + 1) * P], ident)
                    mm.then_inc(probsT_mm, 1)
                if u >= 1:
                    before = u - 1
                    side = before // 2
                    pe.wait_ge(probsT_ready, u)
                    for pair in range(2):
                        c = 2 * side + pair
                        for i in range(2):
                            hp = 2 * (before % 2) + i
                            mm = nc.tensor.matmul(bank[SUM_BANK[side]][hp * 32:(hp + 1) * 32, c * P:(c + 1) * P], md("parmask")[:, hp * 32:(hp + 1) * 32],
                                                  probsT[:, before, (2 * pair + i) * P:(2 * pair + i + 1) * P], start=True, stop=True)
                    mm.then_inc(sums_mm, 1)
                    for pair in range(2):
                        for half in range(2):
                            b = 4 * side + 2 * pair + half
                            for i in range(2):
                                hp = 2 * (before % 2) + i
                                at = (2 * pair + i) * P + half * L
                                mm = nc.tensor.matmul(bank[ATTN_BANK[side]][hp * 32:(hp + 1) * 32, b * L:(b + 1) * L],
                                                      v_heads[:, b, hp * 32:(hp + 1) * 32], probsT[:, before, at:at + L], start=True, stop=True)
                    mm.then_inc(attn_mm, 1)
            for c in range(NC):
                nc.tensor.matmul(bank[PROJ_BANK[c]][:, c * P:(c + 1) * P], md("bv_cols"), md("wprojT"), start=True, stop=False)
            for c in range(NC):
                pe.wait_ge(attn_ready, c // 2 + 1)
                nc.tensor.matmul(bank[PROJ_BANK[c]][:, c * P:(c + 1) * P], attnT[:, c * P:(c + 1) * P], md("wprojT"), start=False, stop=True).then_inc(proj_mm, 1)
            keep_warm(WARM["zhat"], 2)
            for c in range(NC):
                pe.wait_ge(zhat_ready, c + 1)
                nc.tensor.transpose(bank[4 + c // 2][:, c * P:(c + 1) * P], zhat[:, c, :], ident).then_inc(zT_mm, 1)
            keep_warm(WARM["z"], 2)

            def gate_logits():
                pe.wait_ge(wgi_lo_ready, 1)
                for c in range(NC):
                    cols = slice(c * P, (c + 1) * P)
                    dst = bank[6][:, 128 + c * G * E:128 + (c + 1) * G * E]
                    nc.tensor.matmul(dst, z_hi[:, cols], wgi_hi[:], start=True, stop=False)
                    nc.tensor.matmul(dst, z_lo[:, cols], wgi_hi[:], start=False, stop=False)
                    nc.tensor.matmul(dst, z_hi[:, cols], wgi_lo[:], start=False, stop=True)
                pe.wait_ge(zhatT_ready, 2)
                for c in range(NC):
                    mm = nc.tensor.matmul(bank[6][:, c * G:(c + 1) * G], zhatT[:, c * P:(c + 1) * P], ff("wg"), start=True, stop=True)
                mm.then_inc(logits_mm, 1)

            def up(g, s):
                e, c = divmod(s, HC)
                if c == 0:
                    pe.wait_ge(w_hi_ready, g * E + (e + 1))
                    pe.wait_ge(w_lo_ready, g * E + (e + 1))
                reuse(pe, split_done if from_psum(g, s - HC) else relu_done, g * STEPS + (s + 1 - HC))
                cols = slice(c * P, (c + 1) * P)
                nc.tensor.matmul(bank[c][:], w_hi[:, e % WSPLIT, cols], z_hi[:], start=True, stop=False)
                if isinstance(g, int) and s == 0:
                    nc.tensor.matmul(bank[c][:], w_lo[:, e % WSPLIT, cols], z_hi[:], start=False, stop=False)
                    pe.wait_ge(z_lo_ready, 2)
                    nc.tensor.matmul(bank[c][:], w_hi[:, e % WSPLIT, cols], z_lo[:], start=False, stop=True).then_inc(up_done, 1)
                else:
                    nc.tensor.matmul(bank[c][:], w_hi[:, e % WSPLIT, cols], z_lo[:], start=False, stop=False)
                    nc.tensor.matmul(bank[c][:], w_lo[:, e % WSPLIT, cols], z_hi[:], start=False, stop=True).then_inc(up_done, 1)

            def down(g, s):
                e, c = divmod(s, HC)
                pe.wait_ge(split_done, g * STEPS + (s + 1))
                if c == 0:
                    reuse(pe, o_gated_ready, g * E + (e - 1))
                cols = slice(H + c * D, H + (c + 1) * D)
                o = bank[4 + e % 2]
                nc.tensor.matmul(o[:], w_hi[:, e % WSPLIT, cols], h_hi[:, e % 2, c, :], start=(c == 0), stop=False)
                nc.tensor.matmul(o[:], w_hi[:, e % WSPLIT, cols], h_lo[:, e % 2, c, :], start=False, stop=False)
                nc.tensor.matmul(o[:], w_lo[:, e % WSPLIT, cols], h_hi[:, e % 2, c, :], start=False, stop=(c == HC - 1)).then_inc(down_done, 1)

            def back(g):
                pe.wait_ge(o_summed, g * E)
                for c in range(NC):
                    nc.tensor.transpose(bank[6][:, c * P:(c + 1) * P], moe_sumT[:, c * P:(c + 1) * P], ident).then_inc(yT_mm, 1)

            def back_last():
                pe.wait_ge(relu_done, G * STEPS)
                pe.wait_ge(o_summed, G * E - 2)
                pe.wait_ge(o_gated_ready, G * E - 1)
                for c in range(NC):
                    cols = slice(c * P, (c + 1) * P)
                    nc.tensor.matmul(bank[c][:, 0:P], moe_accT[:, cols], ident, start=True, stop=False)
                    nc.tensor.matmul(bank[c][:, 0:P], o_gated[:, (E - 2) % 2, cols], ident, start=False, stop=False)
                    pe.wait_ge(last_gated, c + 1)
                    nc.tensor.matmul(bank[c][:, 0:P], o_gated[:, (E - 1) % 2, cols], ident, start=False, stop=True).then_inc(yT_mm, 1)

            def gates_turn():
                pe.wait_ge(gates_ready, 1)
                for c in range(NC):
                    mm = nc.tensor.transpose(bank[7][0:SETS * E, c * P:(c + 1) * P], gates[:, c].rearrange("p s e -> p (s e)"), ident)
                mm.then_inc(gatesT_mm, 1)

            def out_bias():
                pe.wait_ge(gatesT_ready, 1)
                for c in range(NC):
                    mm = nc.tensor.matmul(bank[7][:, c * P:(c + 1) * P], gatesT[:, c * P:(c + 1) * P],
                                          ffn[0:SETS * E, FFN_AT["gln_b"]], start=True, stop=True)
                mm.then_inc(seed_out_mm, 1)

            def group(g):
                for s in range(STEPS):
                    if isinstance(g, int):
                        if s == 0:
                            pe.wait_ge(z_hi_ready, 2)
                        up(g, s)
                        if s == LOGITS_STEP:
                            gate_logits()
                        if s >= LAG:
                            down(g, s - LAG)
                        if s == GATES_STEP:
                            gates_turn()
                        if s == SEED_STEP:
                            out_bias()
                    else:
                        up(g, s)
                        down(g, s - LAG)
                        if s == BACK_STEP:
                            back(g)

            group(0)
            with pe.Fori(1, G) as g:
                group(g)
            for s in range(-LAG, 0):
                down(G, s)
            back_last()

        @block.scalar
        def _(act):
            chain = [0]

            def link(ins):
                chain[0] += 1
                ins.then_inc(act_chain, 1)
                act.wait_ge(act_chain, chain[0])

            def root(tmp, dst, ready):
                nc.scalar.activation(dst, tmp, ACT.Exp, scale=-0.5).then_inc(ready, 1)

            def split_hi(e):
                nc.scalar.activation(minus_b1[:, e, :], w_stage[:, e, 0:HC], ACT.Copy, scale=-1.0).then_inc(minus_b1_ready, 1)
                nc.scalar.activation(w_hi[:, e % WSPLIT, :], w_stage[:, e, W_AT:], ACT.Copy).then_inc(w_hi_ready, 1)

            act.preload_act_table_set("natural_log_exp_and_others")
            act.wait_ge(constants_set, 1)
            act.wait_ge(noise_ready, 1)
            link(nc.scalar.activation(noise_log[:], noise_abs[:], ACT.Ln, bias=ln_bias[:, 0:1]))
            root(noise_log[:], noise_abs[:], noise_root)

            def gate_exp(half):
                act.wait_ge(cap_ready, half + 1)
                nc.scalar.activation(gate_u[:, half_cols(half)], gate_cap[:, half_cols(half)], ACT.Exp).then_inc(u_ready, 1)

            def gate_copy(half):
                nc.scalar.activation(gate_in[:, half_cols(half)], bank[half][:, 0:N // 2], ACT.Identity, bias=b_noisy[:, 0:1]).then_inc(gate_copied, 1)

            def denominator(half):
                act.wait_ge(n_ready, half + 1)
                link(nc.scalar.activation(gate_cap[:, half_cols(half)], gate_n[:, half_cols(half)], ACT.Ln, bias=ln_bias[:, 1:2]))
                nc.scalar.activation(gate_r[:, half_cols(half)], gate_cap[:, half_cols(half)], ACT.Exp, scale=-1.0).then_inc(denom_inverse, 1)

            gate_exp(0)
            gate_copy(0)
            gate_exp(1)
            gate_copy(1)
            denominator(0)
            denominator(1)
            for e in range(2):
                act.wait_ge(w_landed[e], 16)
                split_hi(e)
            act.wait_ge(ffn_landed, 16)
            nc.scalar.activation(wgi_hi[:], ff("wgi"), ACT.Copy).then_inc(wgi_hi_ready, 1)
            act.wait_ge(var_ready, 1)
            link(nc.scalar.activation(small[:, 1, :], mv[:, :, 1], ACT.Ln, bias=ln_bias[:, 2:3]))
            root(small[:, 1, :], small[:, 2, :], root_ready)
            for half in range(2):
                act.wait_ge(xhatT_mm, 2 * half + 2)
                nc.scalar.activation(xhatT[:, half_cols(half)], bank[6 + half][:, half_cols(half)], ACT.Copy).then_inc(xhatT_ready, 1)
            for e in range(2, WSPLIT):
                act.wait_ge(w_landed[e], 16)
                split_hi(e)
            act.wait_ge(k_ready, 1)
            for h in range(POOL_MASKS, MASKS):
                nc.scalar.activation(k_heads[:, :, h, :], qkT[:, 0, :].rearrange("p (b l) -> p b l", b=IMG), ACT.Copy,
                                     scale=mid[:, MID_AT["headmask"].start + h:MID_AT["headmask"].start + h + 1]).then_inc(k_heads_act, 1)
            for i in range(2):
                act.wait_ge(v_mm, i + 1)
                nc.scalar.activation(v_heads[:, 4 * i:4 * i + 4, :], bank[i][:].rearrange("p (b d) -> p b d", b=4), ACT.Copy).then_inc(v_ready, 1)

            def turned_out(c):
                act.wait_ge(probsT_mm, c + 1)
                nc.scalar.activation(probsT[:, c, :], bank[PT_BANK[c]][:], ACT.Copy).then_inc(probsT_ready, 1)

            def inverse_sums(half):
                cols = slice(half * N // 2, (half + 1) * N // 2)
                act.wait_ge(sums_mm, 2 * half + 2)
                link(nc.scalar.activation(sum_log[:, cols], bank[SUM_BANK[half]][:, cols], ACT.Ln))
                nc.scalar.activation(sum_inv[:, cols], sum_log[:, cols], ACT.Exp, scale=-1.0).then_inc(sums_inverse, 1)

            for c in range(NC):
                act.wait_ge(shifted_ready, c + 1)
                nc.scalar.activation(probs[:, c, :], shifted[:, c, :], ACT.Exp, scale=float(HD) ** -0.5).then_inc(probs_ready, 1)
                if c >= 1:
                    turned_out(c - 1)
            turned_out(NC - 1)
            inverse_sums(0)
            inverse_sums(1)
            act.wait_ge(var_ready, 2)
            nc.scalar.activation(small[:, 2, :], mv[:, :, 1], ACT.Ln, bias=ln_bias[:, 2:3]).then_inc(act_chain, 1)
            chain[0] += 1
            link(nc.scalar.activation(small[:, 3, :], mv[:, :, 1], ACT.Ln, scale=1.0 + EPS, bias=ln_bias[:, 3:4]))
            root(small[:, 2:4, :], small[:, 4:6, :], root_ready)
            for half in range(2):
                act.wait_ge(zT_ready, half + 1)
                nc.scalar.activation(z_hi[:, half_cols(half)], zT[:, half_cols(half)], ACT.Copy).then_inc(z_hi_ready, 1)
            for half in range(2):
                nc.scalar.activation(zhatT[:, half_cols(half)], bank[4 + half][:, half_cols(half)], ACT.Copy).then_inc(zhatT_ready, 1)

            def y_root(g):
                act.wait_ge(y_var_ready, g)
                if isinstance(g, int):
                    act.wait_ge(y_var_ready, g)
                nc.scalar.activation(y_small[:, 1, :], y_mv[:, :, 1], ACT.Ln, bias=ln_bias[:, 2:3]).then_inc(y_root_ready, 1)
                act.wait_ge(y_root_ready, 2 * g - 1)
                nc.scalar.activation(y_small[:, 2, :], y_small[:, 1, :], ACT.Exp, scale=-0.5).then_inc(y_root_ready, 1)

            def group(g):
                for s in range(STEPS):
                    e, c = divmod(s, HC)
                    if isinstance(g, int) and s == GATES_STEP + 1:
                        act.wait_ge(gatesT_mm, 1)
                        nc.scalar.activation(gatesT[:], bank[7][0:SETS * E, :], ACT.Copy).then_inc(gatesT_ready, 1)
                    act.wait_ge(up_done, g * STEPS + (s + 1))
                    reuse(act, split_done, g * STEPS + (s + 1 - RING))
                    high_done = act_hi_done if c in ACT_HIGH else hi_done
                    b1 = w_stage[:, e, c:c + 1]
                    if from_psum(g, s):
                        reuse(act, down_done, g * STEPS + (s + 1 - 2 * HC))
                        nc.scalar.activation(h_hi[:, e % 2, c, :], bank[c][:], ACT.Relu, bias=b1).then_inc(high_done, 1)
                        high_made(act, g, s)
                        act.wait_ge(minus_b1_ready, g * E + (e + 1))
                        nc.scalar.activation(relu[:, s % RING, :], h_hi[:, e % 2, c, :], ACT.Identity, bias=minus_b1[:, e, c:c + 1]).then_inc(relu_done, 1)
                    else:
                        nc.scalar.activation(relu[:, s % RING, :], bank[c][:], ACT.Relu, bias=b1).then_inc(relu_done, 1)
                        if isinstance(g, int) and s < EARLY:
                            act.wait_ge(relu_done, g * STEPS + (s + 1))
                            nc.scalar.activation(h_hi[:, e % 2, c, :], relu[:, s % RING, :], ACT.Copy).then_inc(high_done, 1)
                    if c == 2 and (not isinstance(g, int) or e + AHEAD >= WSPLIT):
                        n = e + AHEAD
                        act.wait_ge(w_landed[n % E], g * 16 + 16 * (1 + n // E))
                        reuse(act, down_done, g * STEPS + HC * (n - WSPLIT + 1))
                        split_hi(n % E)
                    if isinstance(g, int) and s == GAP_STEP:
                        act.wait_ge(gap_ready, 1)
                        nc.scalar.activation(top[:, 5, :], top[:, 4, :], ACT.Exp).then_inc(gap_exp, 1)
                    if s == Y_ROOT_STEP and not isinstance(g, int):
                        y_root(g)

            group(0)
            with act.Fori(1, G) as g:
                group(g)
            y_root(G)

        @block.gpsimd
        def _(pool):
            def split_lo(e):
                nc.gpsimd.tensor_tensor(w_lo[:, e % WSPLIT, :], w_stage[:, e, W_AT:], w_hi[:, e % WSPLIT, :], ALU.subtract).then_inc(w_lo_ready, 1)

            nc.gpsimd.memset(warm[:], 1.0).then_inc(pool_chain, 1)
            nc.gpsimd.memset(ln_bias[:, 0:1], TINY).then_inc(pool_chain, 1)
            nc.gpsimd.memset(ln_bias[:, 1:2], 2.0).then_inc(pool_chain, 1)
            nc.gpsimd.memset(ln_bias[:, 2:3], EPS).then_inc(pool_chain, 1)
            nc.gpsimd.memset(ln_bias[:, 3:4], EPS * EPS).then_inc(pool_chain, 1)
            pool.wait_ge(pool_chain, 5)
            pool.sem_inc(constants_set, 1)
            for half in range(2):
                cols = half_cols(half)
                pool.wait_ge(m_ready, half + 1)
                nc.gpsimd.tensor_tensor(gate_in_inner[:, cols], gate_in_inner[:, cols], gate_n[:, cols], ALU.mult).then_inc(mn_ready, 1)
            for e in range(2):
                pool.wait_ge(w_hi_ready, e + 1)
                split_lo(e)
            pool.wait_ge(wgi_hi_ready, 1)
            nc.gpsimd.tensor_tensor(wgi_lo[:], ff("wgi"), wgi_hi[:], ALU.subtract).then_inc(wgi_lo_ready, 1)
            pool.wait_ge(mid_landed, 16)
            pool.wait_ge(h0_ready, NC)
            nc.gpsimd.tensor_tensor(h0_bproj[:], h0[:], md("bproj").unsqueeze(1).to_broadcast([P, NC, D]), ALU.add).then_inc(h0b_ready, 1)
            pool.wait_ge(k_ready, 1)
            for h in range(POOL_MASKS):
                mask = mid[:, MID_AT["headmask"].start + h:MID_AT["headmask"].start + h + 1]
                nc.gpsimd.tensor_tensor(k_heads[:, :, h, :], qkT[:, 0, :].rearrange("p (b l) -> p b l", b=IMG),
                                        mask.unsqueeze(1).to_broadcast([P, IMG, L]), ALU.mult).then_inc(k_heads_pool, 1)
            for e in range(2, WSPLIT):
                pool.wait_ge(w_hi_ready, e + 1)
                split_lo(e)
            for s in range(EARLY):
                high_made(pool, 0, s)
                nc.gpsimd.tensor_tensor(h_lo[:, s // HC % 2, s % HC, :], relu[:, s % RING, :], h_hi[:, s // HC % 2, s % HC, :], ALU.subtract).then_inc(split_done, 1)

            def sum_output(g, e):
                if isinstance(g, int):
                    g, e = g + e // E, e % E
                pool.wait_ge(o_gated_ready, g * E + (e + 1))
                if not (isinstance(g, int) and g == 0 and e == 0):
                    pool.wait_ge(o_summed, g * E + e)
                pool.sem_inc(held, 1)
                nc.gpsimd.tensor_tensor(moe_sumT[:] if e % E == E - 1 else moe_accT[:], zT[:] if e % E == 0 else moe_accT[:], o_gated[:, e % 2, :], ALU.add).then_inc(o_summed, 1)

            def group(g):
                for e in range(E):
                    if not isinstance(g, int) or e + AHEAD >= WSPLIT:
                        pool.wait_ge(w_hi_ready, g * E + (e + AHEAD + 1))
                        split_lo((e + AHEAD) % E)
                    if not isinstance(g, int) or e >= OUT_LAG:
                        sum_output(g, e - OUT_LAG)

            group(0)
            with pool.Fori(1, G) as g:
                group(g)

        @block.vector
        def _(dve):
            chain = [0]

            def link(ins):
                chain[0] += 1
                ins.then_inc(dve_chain, 1)
                dve.wait_ge(dve_chain, chain[0])

            def newton(ve, y, t, out_):
                link(nc.vector.scalar_tensor_tensor(t, y, -0.5, y, ALU.mult, ALU.mult))
                link(nc.vector.tensor_tensor(t, t, ve, ALU.mult))
                link(nc.vector.scalar_tensor_tensor(out_, t, 1.5, y, ALU.add, ALU.mult))

            def variance():
                for c in range(NC):
                    ins = nc.vector.bn_aggr(mv[:, c, :], stats[:, c, :])
                ins.then_inc(var_ready, 1)

            dve.wait_ge(noise_landed, 16)
            nc.vector.scalar_tensor_tensor(noise_abs[:], tok[:, 0:NOISE], -1.0, tok[:, 0:NOISE], ALU.mult, ALU.max).then_inc(noise_ready, 1)
            dve.wait_ge(noise_root, 1)
            link(nc.vector.tensor_tensor(noise_f[:], tok[:, 0:NOISE], noise_abs[:], ALU.mult))
            f_in = noise_f[:, 0:KF * 2]
            f_out = noise_f[:, KF * 2:KF * 2 + 2]
            f_row = noise_f[:, KF * 2 + 2:NOISE].rearrange("p (w n) -> p w n", w=2)
            w_noise4 = w_noise[:].rearrange("p (k w n) -> p k w n", k=KF, w=2)
            sw4 = tk("sw").rearrange("p (k w n) -> p k w n", k=KF, w=2)
            dve.wait_ge(tok_landed, 16)
            for w in range(2):
                link(nc.vector.tensor_tensor(w_noise4[:, :, w, :], sw4[:, :, w, :], f_row[:, w, :].unsqueeze(1).to_broadcast([P, KF, D]), ALU.mult))
                for k in range(KF):
                    i = 2 * k + w
                    cols = slice(i * D, (i + 1) * D)
                    ins = nc.vector.scalar_tensor_tensor(w_noisy[:, cols], w_noise[:, cols], f_in[:, i:i + 1], tk("w")[:, cols], ALU.mult, ALU.add)
                ins.then_inc(weights_noisy, 1)
            link(nc.vector.tensor_tensor(b_noisy[:], tk("sb"), f_out, ALU.mult))
            link(nc.vector.tensor_tensor(b_noisy[:], b_noisy[:], tk("b"), ALU.add))
            for half in range(2):
                cols = half_cols(half)
                dve.wait_ge(gate_mm, half + 1)
                nc.vector.tensor_scalar(gate_cap[:, cols], bank[half][:, 0:N // 2], b_noisy[:, 0:1], 20.0, ALU.add, ALU.min).then_inc(cap_ready, 1)
            for half in range(2):
                cols = half_cols(half)
                dve.wait_ge(u_ready, half + 1)
                nc.vector.scalar_tensor_tensor(gate_n[:, cols], gate_u[:, cols], 2.0, gate_u[:, cols], ALU.add, ALU.mult).then_inc(n_ready, 1)

            dve.wait_ge(mid_landed, 16)
            nc.vector.tensor_tensor(pe_b3[:], md("pe"), md("b3"), ALU.add).then_inc(pe_b3_ready, 1)

            def gate_inner(half):
                cols = half_cols(half)
                dve.wait_ge(inner_mm, half + 1)
                dve.wait_ge(gate_copied, half + 1)
                dve.wait_ge(n_ready, half + 1)
                nc.vector.scalar_tensor_tensor(gate_in_inner[:, cols], bank[2 + half][:, 0:N // 2], b_noisy[:, 1:2], gate_in[:, cols], ALU.add, ALU.mult).then_inc(m_ready, 1)

            gate_inner(0)
            refine = {}
            for step in range(4):
                for half in range(2):
                    cols = half_cols(half)
                    if (step, half) == (0, 1):
                        gate_inner(1)
                    if step == 0:
                        dve.wait_ge(denom_inverse, half + 1)
                        ins = nc.vector.scalar_tensor_tensor(gate_u[:, cols], gate_n[:, cols], 2.0, gate_r[:, cols], ALU.add, ALU.mult)
                    if step == 1:
                        ins = nc.vector.scalar_tensor_tensor(gate_u[:, cols], gate_u[:, cols], 2.0, gate_r[:, cols], ALU.subtract, ALU.mult)
                    if step == 2:
                        dve.wait_ge(mn_ready, half + 1)
                        nc.vector.scalar_tensor_tensor(gated[:, cols], gate_in_inner[:, cols], -1.0, gate_u[:, cols], ALU.mult, ALU.mult).then_inc(gated_ready, 1)
                    if step < 2:
                        chain[0] += 1
                        ins.then_inc(dve_chain, 1)
                        refine[step, half] = chain[0]
                    nxt = (step, 1) if half == 0 else (step + 1, 0)
                    if nxt[0] in (1, 2):
                        dve.wait_ge(dve_chain, refine[nxt[0] - 1, nxt[1]])
            dve.wait_ge(pe_b3_ready, 1)
            for c in range(NC + 1):
                if c < NC:
                    dve.wait_ge(h0_mm, c + 1)
                    nc.vector.tensor_tensor(h0[:, c], bank[H0_BANK[c]][:, c * P:(c + 1) * P], pe_b3[:], ALU.add).then_inc(h0_ready, 1)
                if c >= 1:
                    dve.wait_ge(h0_ready, c)
                    ins = nc.vector.bn_stats(stats[:, c - 1, :], h0[:, c - 1, :])
            link(ins)
            variance()
            dve.wait_ge(var_ready, 1)
            link(nc.vector.tensor_scalar(small[:, 0, :], mv[:, :, 1], EPS, None, ALU.add))
            dve.wait_ge(root_ready, 1)
            newton(small[:, 0, :], small[:, 2, :], small[:, 3, :], small[:, 6, :])
            for c in range(NC):
                nc.vector.tensor_scalar(xhat[:, c, :], h0[:, c, :], mv[:, c, 0:1], small[:, 6, c:c + 1], ALU.subtract, ALU.mult).then_inc(xhat_ready, 1)
            for i in range(2):
                for n, (table, dst) in enumerate((("cos", rot_a), ("sin", rot_b))):
                    src = 2 * i + n
                    dve.wait_ge(qk_mm, src + 1)
                    nc.vector.scalar_tensor_tensor(dst[:, i, :].rearrange("p (b l) -> p b l", b=IMG), bank[4 + src][:].rearrange("p (b l) -> p b l", b=IMG),
                                                            mid[:, MID_AT["bqkv"].start + src:MID_AT["bqkv"].start + src + 1],
                                                            md(table).unsqueeze(1).to_broadcast([P, IMG, L]), ALU.add, ALU.mult).then_inc(rot_ready, 1)
                dve.wait_ge(rot_ready, 2 * i + 2)
                nc.vector.tensor_tensor(qkT[:, i, :], rot_a[:, i, :], rot_b[:, i, :], ALU.add).then_inc(q_ready if i else k_ready, 1)
            for c in range(NC):
                dve.wait_ge(scores_mm, c + 1)
                s3 = bank[2 + c][:].rearrange("p (h k) -> p h k", h=HEADS)
                link(nc.vector.tensor_reduce(row_max[:, c, :], s3, AX.X, ALU.max))
                nc.vector.tensor_tensor(shifted[:, c, :].rearrange("p (h k) -> p h k", h=HEADS), s3,
                                        wide(row_max[:, c, :].unsqueeze(2), [P, HEADS, L]), ALU.subtract).then_inc(shifted_ready, 1)
            for half in range(2):
                cols = slice(half * N // 2, (half + 1) * N // 2)
                dve.wait_ge(attn_mm, 2 * half + 2)
                dve.wait_ge(sums_inverse, half + 1)
                nc.vector.tensor_tensor(attnT[:, cols], bank[ATTN_BANK[half]][:, cols], sum_inv[:, cols], ALU.mult).then_inc(attn_ready, 1)
            dve.wait_ge(h0b_ready, 1)
            for c in range(NC + 1):
                if c < NC:
                    dve.wait_ge(proj_mm, c + 1)
                    nc.vector.tensor_tensor(h1[:, c], bank[PROJ_BANK[c]][:, c * P:(c + 1) * P], h0_bproj[:, c], ALU.add).then_inc(h1_ready, 1)
                if c >= 1:
                    dve.wait_ge(h1_ready, c)
                    ins = nc.vector.bn_stats(stats[:, c - 1, :], h1[:, c - 1, :])
            link(ins)
            variance()
            dve.wait_ge(var_ready, 2)
            nc.vector.tensor_scalar(small[:, 0, :], mv[:, :, 1], EPS, None, ALU.add).then_inc(dve_chain, 1)
            chain[0] += 1
            link(nc.vector.tensor_scalar(small[:, 1, :], mv[:, :, 1], 1.0 + EPS, EPS * EPS, ALU.mult, ALU.add))
            dve.wait_ge(root_ready, 2)
            newton(small[:, 0:2, :], small[:, 4:6, :], small[:, 2:4, :], small[:, 6:8, :])
            for c in range(NC):
                nc.vector.tensor_scalar(zhat[:, c, :], h1[:, c, :], mv[:, c, 0:1], small[:, 7, c:c + 1], ALU.subtract, ALU.mult).then_inc(zhat_ready, 1)
            dve.wait_ge(ffn_landed, 16)
            for half in range(2):
                cols = half_cols(half)
                dve.wait_ge(zT_mm, 2 * half + 2)
                nc.vector.tensor_scalar(zT[:, cols], bank[4 + half][:, cols], ff("ln_g"), ff("ln_b"), ALU.mult, ALU.add).then_inc(zT_ready, 1)
            for half in range(2):
                cols = half_cols(half)
                dve.wait_ge(z_hi_ready, half + 1)
                nc.vector.tensor_tensor(z_lo[:, cols], zT[:, cols], z_hi[:, cols], ALU.subtract).then_inc(z_lo_ready, 1)
            link(nc.vector.tensor_tensor(small[:, 3, :], small[:, 1, :], small[:, 7, :], ALU.mult))
            link(nc.vector.tensor_tensor(small[:, 3, :], small[:, 3, :], small[:, 6, :], ALU.mult))
            nc.vector.scalar_tensor_tensor(small[:, 4, :], mv[:, :, 0], -1.0, small[:, 6, :], ALU.mult, ALU.mult)
            link(nc.vector.tensor_scalar(small[:, 5, :], small[:, 6, :], 1.0, None, ALU.add))
            for c in range(NC):
                nc.vector.tensor_scalar(out_acc[:, c, :], h1[:, c, :], small[:, 5, c:c + 1], small[:, 4, c:c + 1], ALU.mult, ALU.add).then_inc(out_seeded, 1)
            flat = lambda t: t[:].rearrange("p c s e -> p (c s) e")
            spread = lambda ap: ap.unsqueeze(2).to_broadcast([P, NC * SETS, E])
            order = ff("order").unsqueeze(1).to_broadcast([P, NC * SETS, E])
            chain[0] += 2
            nc.vector.memset(logits[:, :, G, G:E], -1e30).then_inc(dve_chain, 1)
            dve.wait_ge(logits_mm, 1)
            nc.vector.tensor_tensor(logits[:, :, G, 0:G], bank[6][:, 0:NC * G].rearrange("p (c g) -> p c g", c=NC),
                                    small[:, 3, :].unsqueeze(2).to_broadcast([P, NC, G]), ALU.mult).then_inc(dve_chain, 1)
            link(nc.vector.tensor_copy(logits[:].rearrange("p c s e -> p c (s e)")[:, :, 0:G * E],
                                       bank[6][:, 128:128 + NC * G * E].rearrange("p (c x) -> p c x", c=NC)))
            link(nc.vector.tensor_reduce(top[:, 0, :], flat(logits), AX.X, ALU.max))
            link(nc.vector.tensor_tensor(flat(equal), flat(logits), spread(top[:, 0, :]), ALU.is_equal))
            link(nc.vector.tensor_tensor(flat(key), flat(equal), order, ALU.mult))
            link(nc.vector.tensor_reduce(top[:, 1, :], flat(key), AX.X, ALU.max))
            link(nc.vector.tensor_tensor(flat(first), flat(key), spread(top[:, 1, :]), ALU.is_equal))
            link(nc.vector.scalar_tensor_tensor(flat(rest), flat(first), -1e38, flat(logits), ALU.mult, ALU.add))
            link(nc.vector.tensor_reduce(top[:, 2, :], flat(rest), AX.X, ALU.max))
            nc.vector.tensor_tensor(top[:, 4, :], top[:, 2, :], top[:, 0, :], ALU.subtract).then_inc(gap_ready, 1)
            link(nc.vector.tensor_tensor(flat(equal), flat(rest), spread(top[:, 2, :]), ALU.is_equal))
            link(nc.vector.tensor_tensor(flat(key), flat(equal), order, ALU.mult))
            link(nc.vector.tensor_reduce(top[:, 3, :], flat(key), AX.X, ALU.max))
            link(nc.vector.tensor_tensor(flat(second), flat(key), spread(top[:, 3, :]), ALU.is_equal))
            dve.wait_ge(gap_exp, 1)
            link(nc.vector.tensor_scalar(top[:, 6, :], top[:, 5, :], 1.0, None, ALU.add))
            link(nc.vector.reciprocal(top[:, 7, :], top[:, 6, :]))
            link(nc.vector.tensor_tensor(top[:, 6, :], top[:, 5, :], top[:, 7, :], ALU.mult))
            link(nc.vector.tensor_tensor(flat(first), flat(first), spread(top[:, 7, :]), ALU.mult))
            link(nc.vector.tensor_tensor(flat(second), flat(second), spread(top[:, 6, :]), ALU.mult))
            nc.vector.tensor_tensor(flat(gates), flat(first), flat(second), ALU.add).then_inc(gates_ready, 1)

            def seed_out():
                dve.wait_ge(out_seeded, NC)
                dve.wait_ge(seed_out_mm, 1)
                link(nc.vector.tensor_tensor(out_acc[:], bank[7][:].rearrange("p (c d) -> p c d", c=NC), out_acc[:], ALU.add))

            def high(g, s):
                e, c = divmod(s, HC)
                dve.wait_ge(relu_done, g * STEPS + (s + 1))
                reuse(dve, down_done, g * STEPS + (s + 1 - 2 * HC))
                nc.vector.tensor_copy(h_hi[:, e % 2, c, :], relu[:, s % RING, :]).then_inc(hi_done, 1)

            def low(g, s):
                e, c = divmod(s, HC)
                high_made(dve, g, s)
                if from_psum(g, s):
                    dve.wait_ge(relu_done, g * STEPS + (s + 1))
                    dve.wait_ge(minus_b1_ready, g * E + (e + 1))
                    nc.vector.scalar_tensor_tensor(h_lo[:, e % 2, c, :], bank[c][:], minus_b1[:, e, c:c + 1], relu[:, s % RING, :],
                                                   ALU.max, ALU.subtract).then_inc(split_done, 1)
                else:
                    nc.vector.tensor_tensor(h_lo[:, e % 2, c, :], relu[:, s % RING, :], h_hi[:, e % 2, c, :], ALU.subtract).then_inc(split_done, 1)

            def gate_last():
                dve.wait_ge(down_done, G * STEPS)
                dve.wait_ge(iw_landed[E - 1], G * 16)
                dve.wait_ge(o_summed, G * E - 2)
                for c in range(NC):
                    cols = slice(c * P, (c + 1) * P)
                    nc.vector.scalar_tensor_tensor(o_gated[:, (E - 1) % 2, cols], bank[4 + (E - 1) % 2][:, cols], w_stage[:, E - 1, B2_AT:B2_AT + 1],
                                                   iw_rows[:, E - 1, cols], ALU.add, ALU.mult).then_inc(last_gated, 1)

            def gate_output(g, e):
                dve.wait_ge(down_done, g * STEPS + HC * (e + 1))
                dve.wait_ge(iw_landed[e % E], g * 16 + (16 if e >= 0 else 0))
                reuse(dve, o_summed, g * E + (e - 1))
                nc.vector.scalar_tensor_tensor(o_gated[:, e % 2, :], bank[4 + e % 2][:], w_stage[:, e % E, B2_AT:B2_AT + 1], iw_rows[:, e % E, :], ALU.add, ALU.mult).then_inc(o_gated_ready, 1)

            def y_chunk(g, c):
                return bank[c][:, 0:P] if isinstance(g, int) else bank[6][:, c * P:(c + 1) * P]

            YLINKS = 8
            Y_PARTS = 5
            Y_AT = {13: 0, 15: 1, 18: 2, 21: 3, 24: 4}

            def y_link(ins, g, n):
                ins.then_inc(yT_read, 1)
                dve.wait_ge(yT_read, g * YLINKS + (n + 1 - YLINKS))

            def y_out(g, part):
                if part == 0:
                    for c in range(NC):
                        dve.wait_ge(yT_mm, (g - 1) * NC + (c + 1) if isinstance(g, int) else g * NC)
                        ins = nc.vector.bn_stats(y_stats[:, c, :], y_chunk(g, c))
                    y_link(ins, g, 0)
                if part == 1:
                    dve.sem_inc(held, 1)
                    for c in range(NC):
                        ins = nc.vector.bn_aggr(y_mv[:, c, :], y_stats[:, c, :])
                    ins.then_inc(y_var_ready, 1)
                    dve.wait_ge(y_var_ready, g)
                    y_link(nc.vector.tensor_scalar(y_small[:, 0, :], y_mv[:, :, 1], EPS, None, ALU.add), g, 1)
                if part == 2:
                    for c in range(NC):
                        if isinstance(g, int):
                            gain = ffn[:, FFN_AT["gln_g"].start + (g - 1) * D:FFN_AT["gln_g"].start + g * D]
                        else:
                            gain = ff("gln_g").rearrange("p (g d) -> p g d", g=G)[:, bass.ds(g - 1, 1), :].rearrange("p a d -> p (a d)")
                        ins = nc.vector.scalar_tensor_tensor(y_gain[:, c, :], y_chunk(g, c), y_mv[:, c, 0:1], gain, ALU.subtract, ALU.mult)
                    y_link(ins, g, 2)
                if part == 3:
                    dve.wait_ge(y_root_ready, 2 * g)
                    y = y_small[:, 2, :]
                    if isinstance(g, int):
                        gw = gates[:, :, G, g - 1]
                    else:
                        gw = gates[:, :, G, bass.ds(g - 1, 1)].rearrange("p c a -> p (c a)")
                    y_link(nc.vector.scalar_tensor_tensor(y_small[:, 3, :], y, -0.5, y, ALU.mult, ALU.mult), g, 3)
                    nc.vector.tensor_tensor(y_small[:, 4, :], y, gw, ALU.mult).then_inc(yT_read, 1)
                    y_link(nc.vector.tensor_tensor(y_small[:, 3, :], y_small[:, 3, :], y_small[:, 0, :], ALU.mult), g, 5)
                    y_link(nc.vector.scalar_tensor_tensor(y_small[:, 5, :], y_small[:, 3, :], 1.5, y_small[:, 4, :], ALU.add, ALU.mult), g, 6)
                if part == 4:
                    for c in range(NC):
                        ins = nc.vector.scalar_tensor_tensor(out_acc[:, c, :], y_gain[:, c, :], y_small[:, 5, c:c + 1], out_acc[:, c, :], ALU.mult, ALU.add)
                        if isinstance(g, int) and c < NC - 1:
                            ins.then_inc(out_ready, 1)
                    y_link(ins, g, 7)

            def group(g):
                for s in range(STEPS):
                    if isinstance(g, int) and s < EARLY:
                        continue
                    if isinstance(g, int) and s == EARLY:
                        dve.wait_ge(split_done, EARLY)
                    if s % HC not in ACT_HIGH:
                        high(g, s)
                    low(g, s)
                    if isinstance(g, int):
                        if s == SEED_STEP + 2:
                            seed_out()
                    if s % HC == 2 and (s >= 2 * HC or not isinstance(g, int)):
                        gate_output(g, s // HC - 2)
                    if not isinstance(g, int) and s in Y_AT:
                        y_out(g, Y_AT[s])

            group(0)
            with dve.Fori(1, G) as g:
                group(g)
            gate_output(G, -2)
            gate_last()
            for part in range(Y_PARTS):
                y_out(G, part)
            nc.vector.engine_nop().then_inc(out_ready, 1)


def shape_tables():
    pos = np.arange(L, dtype=np.float32)[:, None]
    div = np.exp(np.arange(0, D, 2, dtype=np.float32) * np.float32(-np.log(10000.0) / D)).astype(np.float32)
    ang = (pos * div).astype(np.float32)
    pe = np.stack([np.sin(ang), np.cos(ang)], axis=-1).reshape(L, D).astype(np.float32)
    freqs = (1.0 / np.float32(10000.0) ** (np.arange(0, HD, 2, dtype=np.float32) / HD)).astype(np.float32)
    turn = np.outer(np.arange(L, dtype=np.float32), freqs).astype(np.float32)
    dim = np.arange(D) % HD
    cos = np.cos(turn)[:, dim // 2].T.astype(np.float32)
    sin = (np.sin(turn)[:, dim // 2].T * np.where(dim % 2 == 0, -1.0, 1.0)[:, None]).astype(np.float32)
    p = np.arange(P)
    headmask = (p[:, None] // HD % MASKS == np.arange(MASKS)[None, :]).astype(np.float32)
    parmask = (p[:, None] // L == (np.arange(D)[None, :] // HD) % 2).astype(np.float32)
    order = np.tile(np.arange(E, 0, -1, dtype=np.float32), (P, 1))
    return {"pe": np.concatenate([pe] * (P // L)), "cos": cos, "sin": sin, "headmask": headmask,
            "parmask": parmask, "order": order, "ident": np.eye(P, dtype=np.float32)}


def kernel(**inputs):
    import concourse.bacc as bacc
    from concourse.bass_utils import run_bass_kernel_spmd

    a = {k: np.asarray(v) for k, v in inputs.items()}
    t = shape_tables()

    def rows(v):
        return np.broadcast_to(v.reshape(1, -1), (P, v.size))

    def pack(parts, values):
        return np.ascontiguousarray(np.concatenate([values[n].reshape(P, w) for n, w in parts], axis=1))

    def feat(wa, wb):
        return np.stack([wa, wb]).reshape(2, D, KF, P).transpose(3, 2, 0, 1)

    x = a["x"].reshape(IMG, SIDE, PATCH, SIDE, PATCH).transpose(2, 4, 0, 1, 3).reshape(KF, P, N).transpose(1, 0, 2)
    tok = {
        "noise_in": np.stack([a["L0_tok_eps_in1"], a["L0_tok_eps_in2"]]).reshape(2, KF, P).transpose(2, 1, 0),
        "noise_out": np.stack([a["L0_tok_eps_out1"], a["L0_tok_eps_out2"]], axis=1),
        "noise_row": rows(np.stack([a["L0_tok_eps_out1"], a["L0_tok_eps_out2"]])),
        "b": np.stack([a["L0_tok_W1_b"], a["L0_tok_W2_b"]], axis=1),
        "sb": np.stack([a["L0_tok_W1_sb"], a["L0_tok_W2_sb"]], axis=1),
        "w": feat(a["L0_tok_W1_w"], a["L0_tok_W2_w"]),
        "sw": feat(a["L0_tok_W1_sw"], a["L0_tok_W2_sw"]),
    }
    swap = np.arange(D) ^ 1
    wq, wk, wv = a["L0_attn_Wqkv"].reshape(3, D, D)
    bq, bk, bv = a["L0_attn_bqkv"].reshape(3, D)
    wv_parity = np.zeros((D, 2, HEADS // 2, 2, HD), np.float32)
    for parity in range(2):
        wv_parity[:, parity, :, parity] = wv.T.reshape(D, HEADS // 2, 2, HD)[:, :, parity]
    mid = {
        "w3T": a["L0_tok_W3_w"].T, "b3": rows(a["L0_tok_W3_b"]), "pe": t["pe"], "ident": t["ident"],
        "wqkvT": np.concatenate([wk.T, wk[swap].T, wq.T, wq[swap].T, wv_parity.reshape(D, 2 * D)], axis=1),
        "bqkv": np.stack([bk, bk[swap], bq, bq[swap]], axis=1), "bv_cols": np.broadcast_to(bv.reshape(-1, 1), (D, P)),
        "cos": t["cos"], "sin": t["sin"], "headmask": t["headmask"], "parmask": t["parmask"],
        "wprojT": a["L0_attn_Wproj"].T, "bproj": rows(a["L0_attn_bproj"]),
    }
    gln_b = np.zeros((P, D), np.float32)
    gln_b[G * E:G * E + G] = a["L0_ffn_gln_b"]
    ffn = {
        "wg": a["L0_ffn_wg_group"], "wgi": a["L0_ffn_wg_inner"].transpose(1, 0, 2), "ln_g": a["L0_ffn_ln_g"],
        "ln_b": a["L0_ffn_ln_b"], "order": t["order"], "gln_g": rows(a["L0_ffn_gln_g"]), "gln_b": gln_b,
    }
    experts = np.concatenate([
        a["L0_ffn_b1"].reshape(G * E, HC, P).transpose(0, 2, 1),
        a["L0_ffn_b2"].reshape(G * E, D, 1), np.zeros((G * E, P, W_AT - HC - 1), np.float32),
        a["L0_ffn_W1"].reshape(G * E, D, H),
        a["L0_ffn_W2"].reshape(G * E, HC, P, D).transpose(0, 2, 1, 3).reshape(G * E, P, H)], axis=2)
    arrays = {"tok_in": pack(TOK_PARTS, tok), "x_in": np.ascontiguousarray(x), "mid_in": pack(MID_PARTS, mid), "ffn_in": pack(FFN_PARTS, ffn),
              "experts_in": np.ascontiguousarray(experts)}

    nc = bacc.Bacc("TRN2", target_bir_lowering=False, num_devices=1)
    args = [nc.dram_tensor(n, v.shape, F32, kind="ExternalInput").ap() for n, v in arrays.items()]
    out = nc.dram_tensor("out", (N, D), F32, kind="ExternalOutput").ap()
    vit_tower(nc, *args, out)
    r = run_bass_kernel_spmd(nc, [arrays], core_ids=[0])
    return r.results[0]["out"].reshape(IMG, L, D)
```
